# Optimizing a Trainium2 kernel written in Bass

```python
import numpy as np
import jax
import jax.numpy as jnp

def _softmax(x, axis=-1):
    return jax.nn.softmax(x, axis=axis)

def _gelu(x):
    return jax.nn.gelu(x, approximate=True)

def _silu(x):
    return jax.nn.silu(x)

def _sigmoid(x):
    return jax.nn.sigmoid(x)

def _layernorm(x, axis=-1, eps=1e-05):
    m = jnp.mean(x, axis=axis, keepdims=True)
    v = jnp.var(x, axis=axis, keepdims=True)
    return (x - m) / jnp.sqrt(v + eps)

def _scatter_add(tgt, idx, src, axis=0):
    return tgt.at[idx].add(src)

def _segment_sum(src, seg, n):
    return jax.ops.segment_sum(src, seg, n)
kernel_name = 'mk_xattn_seq_d2_seqx_r4_a7b5fe'

def setup_inputs(seed: int=0):
    np.random.seed(seed)
    _w = jnp.asarray

    def _rec_inputs():
        import jax
        import jax.numpy as jnp
        _rk = jax.random.key(seed)
        x = -0.0002928 + 1 * jax.random.normal(jax.random.fold_in(_rk, 1), (16, 128, 512), jnp.float32)
        _lenS = 128 - jax.random.randint(jax.random.fold_in(_rk, 7), (16,), 0, max(1, 128 // 4) + 1, jnp.int32)
        _lenS2 = 128 - jax.random.randint(jax.random.fold_in(_rk, 8), (16,), 0, max(1, 128 // 4) + 1, jnp.int32)
        _ctx_2048P = jax.random.normal(jax.random.fold_in(_rk, 11), (16, 16, 512), jnp.float32)
        _ctx_2048c = jax.random.dirichlet(jax.random.fold_in(_rk, 511), 0.3 * jnp.ones((16,), jnp.float32), (16, 128))
        _ctx_2048t = jnp.einsum('bsk,bkd->bsd', _ctx_2048c, _ctx_2048P)
        _ctx_2048t = _ctx_2048t * jax.lax.rsqrt(jnp.mean(jnp.square(_ctx_2048t)) + 1e-12) * 0.953939
        ctx_2048 = -1.39393e-06 + 0.999914 * (_ctx_2048t + 0.3 * jax.random.normal(jax.random.fold_in(_rk, 611), (16, 128, 512), jnp.float32))
        _validS = jnp.arange(128)[None, :] < _lenS[:, None]
        _validS2 = jnp.arange(128)[None, :] < _lenS2[:, None]
        _causal = jnp.tril(jnp.ones((128, 128), dtype=bool))
        mask_1x1xSxS2_fc1 = jnp.where(jnp.broadcast_to(_validS2[0:1, None, None, :], (1, 1, 128, 128)), 1.0, 0.0).astype(jnp.float32)
        mask_Bx1xSxS2_ff1 = jnp.where(jnp.ones((16, 1, 128, 128), dtype=bool), 1.0, 0.0).astype(jnp.float32)
        mask_BxS2_bf1 = jnp.ones((16, 128), dtype=bool)
        return (x, ctx_2048, mask_1x1xSxS2_fc1, mask_Bx1xSxS2_ff1, mask_BxS2_bf1)
    x, ctx_2048, mask_1x1xSxS2_fc1, mask_Bx1xSxS2_ff1, mask_BxS2_bf1 = _rec_inputs()

    def _L0_xattn_setup():
        import jax, jax.numpy as jnp
        import numpy as np
        H = 512
        NH = 16
        HD = H // NH
        EPS = 1e-05

        def gelu(x):
            return 0.5 * x * (1.0 + jnp.tanh(0.7978845608028654 * x * (1.0 + 0.044715 * x * x)))

        def layernorm(x, scale, bias):
            m = jnp.mean(x, axis=-1, keepdims=True)
            v = jnp.mean(jnp.square(x - m), axis=-1, keepdims=True)
            return (x - m) * jax.lax.rsqrt(v + EPS) * scale + bias

        def split_heads(x):
            b, s, _ = x.shape
            return x.reshape(b, s, NH, HD).transpose(0, 2, 1, 3)

        def merge_heads(x):
            b, nh, s, hd = x.shape
            return x.transpose(0, 2, 1, 3).reshape(b, s, nh * hd)

        def attention(q, k, v, mask):
            scores = jnp.einsum('bhqd,bhkd->bhqk', q, k) / jnp.sqrt(jnp.float32(HD))
            scores = scores * mask - 10000.0 * (1.0 - mask)
            probs = jax.nn.softmax(scores, axis=-1)
            return jnp.einsum('bhqk,bhkd->bhqd', probs, v)
        key = jax.random.key(seed)
        ks = jax.random.split(key, 16)
        b, s, t = (2, 256, 256)
        w = lambda k, i, o: jax.random.normal(k, (i, o), jnp.float32) * 0.02
        inp = {'hidden_states': jax.random.normal(ks[0], (b, s, H), jnp.float32), 'encoder_states': jax.random.normal(ks[1], (b, t, H), jnp.float32), 'ltor_mask': jnp.tril(jnp.ones((1, 1, s, s), jnp.float32)), 'cross_mask': jnp.ones((b, 1, s, t), jnp.float32), 'ln1_s': jnp.ones((H,), jnp.float32), 'ln1_b': jnp.zeros((H,), jnp.float32), 'w_qkv': w(ks[2], H, 3 * H), 'b_qkv': jnp.zeros((3 * H,), jnp.float32), 'w_ao': w(ks[3], H, H), 'b_ao': jnp.zeros((H,), jnp.float32), 'ln2_s': jnp.ones((H,), jnp.float32), 'ln2_b': jnp.zeros((H,), jnp.float32), 'w_q': w(ks[4], H, H), 'b_q': jnp.zeros((H,), jnp.float32), 'w_kv': w(ks[5], H, 2 * H), 'b_kv': jnp.zeros((2 * H,), jnp.float32), 'w_co': w(ks[6], H, H), 'b_co': jnp.zeros((H,), jnp.float32), 'ln3_s': jnp.ones((H,), jnp.float32), 'ln3_b': jnp.zeros((H,), jnp.float32), 'w1': w(ks[7], H, 4 * H), 'b1': jnp.zeros((4 * H,), jnp.float32), 'w2': w(ks[8], 4 * H, H), 'b2': jnp.zeros((H,), jnp.float32)}
        return inp
    _L0_xattn_all = _L0_xattn_setup()
    _L0_xattn_in = {k: v for k, v in _L0_xattn_all.items() if k in ('ln1_s', 'ln1_b', 'w_qkv', 'b_qkv', 'w_ao', 'b_ao', 'ln2_s', 'ln2_b', 'w_q', 'b_q', 'w_kv', 'b_kv', 'w_co', 'b_co', 'ln3_s', 'ln3_b', 'w1', 'b1', 'w2', 'b2')}
    del _L0_xattn_all

    def _L1_xattn_setup():
        import jax, jax.numpy as jnp
        import numpy as np
        HIDDEN = 512
        HEADS = 16
        HEAD_DIM = HIDDEN // HEADS
        LN_EPS = 1e-05
        GATE_INIT = 0.5

        def _layer_norm(x, gamma, beta):
            mu = jnp.mean(x, axis=-1, keepdims=True)
            var = jnp.mean(jnp.square(x - mu), axis=-1, keepdims=True)
            return (x - mu) * jax.lax.rsqrt(var + LN_EPS) * gamma + beta
        key = jax.random.key(seed)
        ks = jax.random.split(key, 8)
        B, T_TEXT, T_AUDIO = (4, 512, 375)
        s = 0.02
        return {'hidden_states': jax.random.normal(ks[0], (B, T_TEXT, HIDDEN), jnp.float32), 'audio_kv': jax.random.normal(ks[1], (B, T_AUDIO, HIDDEN), jnp.float32), 'audio_attention_mask': jnp.ones((B, T_AUDIO), dtype=bool), 'Wq': jax.random.normal(ks[2], (HIDDEN, HIDDEN), jnp.float32) * s, 'Wk': jax.random.normal(ks[3], (HIDDEN, HIDDEN), jnp.float32) * s, 'Wv': jax.random.normal(ks[4], (HIDDEN, HIDDEN), jnp.float32) * s, 'Wo': jax.random.normal(ks[5], (HIDDEN, HIDDEN), jnp.float32) * s, 'ln_gamma': jnp.ones((HIDDEN,), jnp.float32), 'ln_beta': jnp.zeros((HIDDEN,), jnp.float32), 'gate': jnp.array([GATE_INIT], jnp.float32)}
    _L1_xattn_all = _L1_xattn_setup()
    _L1_xattn_in = {k: v for k, v in _L1_xattn_all.items() if k in ('Wq', 'Wk', 'Wv', 'Wo', 'ln_gamma', 'ln_beta', 'gate')}
    del _L1_xattn_all
    return {'x': x, 'ctx_2048': ctx_2048, 'mask_1x1xSxS2_fc1': mask_1x1xSxS2_fc1, 'mask_Bx1xSxS2_ff1': mask_Bx1xSxS2_ff1, 'mask_BxS2_bf1': mask_BxS2_bf1, 'L0_xattn_ln1_s': _L0_xattn_in['ln1_s'], 'L0_xattn_ln1_b': _L0_xattn_in['ln1_b'], 'L0_xattn_w_qkv': _L0_xattn_in['w_qkv'], 'L0_xattn_b_qkv': _L0_xattn_in['b_qkv'], 'L0_xattn_w_ao': _L0_xattn_in['w_ao'], 'L0_xattn_b_ao': _L0_xattn_in['b_ao'], 'L0_xattn_ln2_s': _L0_xattn_in['ln2_s'], 'L0_xattn_ln2_b': _L0_xattn_in['ln2_b'], 'L0_xattn_w_q': _L0_xattn_in['w_q'], 'L0_xattn_b_q': _L0_xattn_in['b_q'], 'L0_xattn_w_kv': _L0_xattn_in['w_kv'], 'L0_xattn_b_kv': _L0_xattn_in['b_kv'], 'L0_xattn_w_co': _L0_xattn_in['w_co'], 'L0_xattn_b_co': _L0_xattn_in['b_co'], 'L0_xattn_ln3_s': _L0_xattn_in['ln3_s'], 'L0_xattn_ln3_b': _L0_xattn_in['ln3_b'], 'L0_xattn_w1': _L0_xattn_in['w1'], 'L0_xattn_b1': _L0_xattn_in['b1'], 'L0_xattn_w2': _L0_xattn_in['w2'], 'L0_xattn_b2': _L0_xattn_in['b2'], 'L1_xattn_Wq': _L1_xattn_in['Wq'], 'L1_xattn_Wk': _L1_xattn_in['Wk'], 'L1_xattn_Wv': _L1_xattn_in['Wv'], 'L1_xattn_Wo': _L1_xattn_in['Wo'], 'L1_xattn_ln_gamma': _L1_xattn_in['ln_gamma'], 'L1_xattn_ln_beta': _L1_xattn_in['ln_beta'], 'L1_xattn_gate': _L1_xattn_in['gate']}

def reference(x, ctx_2048, mask_1x1xSxS2_fc1, mask_Bx1xSxS2_ff1, mask_BxS2_bf1, L0_xattn_ln1_s, L0_xattn_ln1_b, L0_xattn_w_qkv, L0_xattn_b_qkv, L0_xattn_w_ao, L0_xattn_b_ao, L0_xattn_ln2_s, L0_xattn_ln2_b, L0_xattn_w_q, L0_xattn_b_q, L0_xattn_w_kv, L0_xattn_b_kv, L0_xattn_w_co, L0_xattn_b_co, L0_xattn_ln3_s, L0_xattn_ln3_b, L0_xattn_w1, L0_xattn_b1, L0_xattn_w2, L0_xattn_b2, L1_xattn_Wq, L1_xattn_Wk, L1_xattn_Wv, L1_xattn_Wo, L1_xattn_ln_gamma, L1_xattn_ln_beta, L1_xattn_gate):
    import jax
    import jax.numpy as jnp

    def _L0_xattn_ref(hidden_states, encoder_states, ltor_mask, cross_mask, ln1_s, ln1_b, w_qkv, b_qkv, w_ao, b_ao, ln2_s, ln2_b, w_q, b_q, w_kv, b_kv, w_co, b_co, ln3_s, ln3_b, w1, b1, w2, b2):
        import jax, jax.numpy as jnp
        import numpy as np
        H = 512
        NH = 16
        HD = H // NH
        EPS = 1e-05

        def gelu(x):
            return 0.5 * x * (1.0 + jnp.tanh(0.7978845608028654 * x * (1.0 + 0.044715 * x * x)))

        def layernorm(x, scale, bias):
            m = jnp.mean(x, axis=-1, keepdims=True)
            v = jnp.mean(jnp.square(x - m), axis=-1, keepdims=True)
            return (x - m) * jax.lax.rsqrt(v + EPS) * scale + bias

        def split_heads(x):
            b, s, _ = x.shape
            return x.reshape(b, s, NH, HD).transpose(0, 2, 1, 3)

        def merge_heads(x):
            b, nh, s, hd = x.shape
            return x.transpose(0, 2, 1, 3).reshape(b, s, nh * hd)

        def attention(q, k, v, mask):
            scores = jnp.einsum('bhqd,bhkd->bhqk', q, k) / jnp.sqrt(jnp.float32(HD))
            scores = scores * mask - 10000.0 * (1.0 - mask)
            probs = jax.nn.softmax(scores, axis=-1)
            return jnp.einsum('bhqk,bhkd->bhqd', probs, v)
        ln_out = layernorm(hidden_states, ln1_s, ln1_b)
        qkv = ln_out @ w_qkv + b_qkv
        q, k, v = jnp.split(qkv, 3, axis=-1)
        ctx = merge_heads(attention(split_heads(q), split_heads(k), split_heads(v), ltor_mask))
        attn_out = ctx @ w_ao + b_ao
        x = hidden_states + attn_out
        ln_out = layernorm(x, ln2_s, ln2_b)
        q = ln_out @ w_q + b_q
        kv = encoder_states @ w_kv + b_kv
        k, v = jnp.split(kv, 2, axis=-1)
        ctx = merge_heads(attention(split_heads(q), split_heads(k), split_heads(v), cross_mask))
        cross_out = ctx @ w_co + b_co
        x = x + cross_out
        ln_out = layernorm(x, ln3_s, ln3_b)
        mlp_out = gelu(ln_out @ w1 + b1) @ w2 + b2
        return x + mlp_out

    def _L1_xattn_ref(hidden_states, audio_kv, audio_attention_mask, Wq, Wk, Wv, Wo, ln_gamma, ln_beta, gate):
        import jax, jax.numpy as jnp
        import numpy as np
        HIDDEN = 512
        HEADS = 16
        HEAD_DIM = HIDDEN // HEADS
        LN_EPS = 1e-05
        GATE_INIT = 0.5

        def _layer_norm(x, gamma, beta):
            mu = jnp.mean(x, axis=-1, keepdims=True)
            var = jnp.mean(jnp.square(x - mu), axis=-1, keepdims=True)
            return (x - mu) * jax.lax.rsqrt(var + LN_EPS) * gamma + beta
        B, Tt, D = hidden_states.shape
        Ta = audio_kv.shape[1]
        scale = HEAD_DIM ** (-0.5)
        a = _layer_norm(audio_kv, ln_gamma, ln_beta)
        Q = (hidden_states @ Wq.T).reshape(B, Tt, HEADS, HEAD_DIM).transpose(0, 2, 1, 3)
        K = (a @ Wk.T).reshape(B, Ta, HEADS, HEAD_DIM).transpose(0, 2, 1, 3)
        V = (a @ Wv.T).reshape(B, Ta, HEADS, HEAD_DIM).transpose(0, 2, 1, 3)
        scores = jnp.einsum('bhtd,bhsd->bhts', Q, K) * scale
        mask = audio_attention_mask[:, None, None, :]
        scores = jnp.where(mask, scores, jnp.float32(-jnp.inf))
        attn = jax.nn.softmax(scores, axis=-1)
        out = jnp.einsum('bhts,bhsd->bhtd', attn, V)
        out = out.transpose(0, 2, 1, 3).reshape(B, Tt, D)
        out = out @ Wo.T
        return hidden_states + jnp.tanh(gate) * out
    x = _L0_xattn_ref(x, ctx_2048, mask_1x1xSxS2_fc1, mask_Bx1xSxS2_ff1, L0_xattn_ln1_s, L0_xattn_ln1_b, L0_xattn_w_qkv, L0_xattn_b_qkv, L0_xattn_w_ao, L0_xattn_b_ao, L0_xattn_ln2_s, L0_xattn_ln2_b, L0_xattn_w_q, L0_xattn_b_q, L0_xattn_w_kv, L0_xattn_b_kv, L0_xattn_w_co, L0_xattn_b_co, L0_xattn_ln3_s, L0_xattn_ln3_b, L0_xattn_w1, L0_xattn_b1, L0_xattn_w2, L0_xattn_b2)
    x = _L1_xattn_ref(x, ctx_2048, mask_BxS2_bf1, L1_xattn_Wq, L1_xattn_Wk, L1_xattn_Wv, L1_xattn_Wo, L1_xattn_ln_gamma, L1_xattn_ln_beta, L1_xattn_gate)
    return x

_drawn_inputs = setup_inputs


def setup_inputs(seed=0):
    import zlib

    import numpy as np

    out = dict(_drawn_inputs(seed))
    spreads = {'L0_xattn_ln1_s': (1.0, 0.2),
     'L0_xattn_ln1_b': (0.0, 0.418),
     'L0_xattn_b_qkv': (0.0, 0.1),
     'L0_xattn_b_ao': (0.0, 0.1),
     'L0_xattn_ln2_s': (1.0, 0.6),
     'L0_xattn_ln2_b': (0.0, 2.0),
     'L0_xattn_b_q': (0.0, 2.0),
     'L0_xattn_b_kv': (0.0, 0.1),
     'L0_xattn_b_co': (0.0, 0.1),
     'L0_xattn_ln3_s': (1.0, 0.2),
     'L0_xattn_ln3_b': (0.0, 0.337),
     'L0_xattn_b1': (0.0, 0.1),
     'L0_xattn_b2': (0.0, 0.1),
     'L1_xattn_ln_gamma': (1.0, 0.6),
     'L1_xattn_ln_beta': (0.0, 0.8)}
    factors = {'L0_xattn_w_q': 64.0, 'L1_xattn_Wq': 8.0, 'L1_xattn_Wk': 8.0}
    for name, (base, spread) in spreads.items():
        noise = np.random.default_rng([zlib.crc32(name.encode()), seed]).standard_normal(out[name].shape)
        drawn = base * np.exp(spread * noise) if base else spread * noise
        out[name] = jnp.asarray(drawn.astype(out[name].dtype))
    for name, factor in factors.items():
        out[name] = (out[name] * factor).astype(out[name].dtype)
    return out
```

```python
from contextlib import ExitStack

import concourse.bass as bass
from concourse import mybir

NB, T, H = 16, 128, 512
NH, HD = 16, 32
KC = H // 128
GB = 2
GT = GB * T
NG = NB // GB
FF = 4 * H
NPAIR = FF // 256
SLOTS = 8
STG = 4
EPS = 1e-5
SCALE = float(HD) ** -0.5
GELU_A, GELU_C = 0.044715, 0.7978845608028654

UNITS = {"A": dict(q=0, k=1, v=2, o=3), "B": dict(q=4, k=5, v=6, o=7), "D": dict(k=16, v=17, q=18, o=19)}
W1_UNIT = [8, 10, 12, 14]
W2_UNIT = [9, 11, 13, 15]
COL = dict(ln1_s=0, ln1_b=4, ln2_s=8, ln2_b=12, ln3_s=16, ln3_b=20, lna_s=24, lna_b=28,
           A_q=32, A_k=36, B_q=40, B_k=44, b1=48)
NCOL = 48 + FF // 128
ROW = dict(A_v=0, A_o=1, B_v=2, B_o=3, C_o=4)
ROW_SLOT = dict(A_v=0, A_o=1, B_v=0, B_o=2, C_o=1)


class Mark:

    def __init__(self, counter, value):
        self.counter, self.value = counter, value


class Counter:

    def __init__(self, sem, strides):
        self.sem, self.n, self.strides = sem, 0, strides


class Marks:

    def __init__(self, nc, ctx):
        self.nc, self.ctx = nc, ctx
        self.counters, self.made = [], []
        self.loop = None
        self.waited = {}

    def counter(self, name, attention=0, hidden=0):
        c = Counter(self.ctx.enter_context(self.nc.semaphore(name)), dict(attention=attention, hidden=hidden))
        c.name = name
        self.counters.append(c)
        return c

    def now(self, *counters):
        return [Mark(c, c.n) for c in counters]

    def up(self, instruction, counter, by=1):
        instruction.then_inc(counter.sem, by)
        counter.n += by
        mark = Mark(counter, counter.n)
        if self.loop:
            self.made.append(mark)
        return mark

    def wait(self, engine, *marks):
        for mark in marks:
            if mark is None:
                continue
            c = mark.counter
            key = (engine.engine, c.name)
            if self.waited.get(key, 0) >= mark.value:
                continue
            self.waited[key] = mark.value
            value = mark.value
            if self.loop and c.strides[self.loop[1]]:
                self.moving.add(c.name)
                assert mark.value > 0, c.name
                value = self.loop[0] * c.strides[self.loop[1]] + value
            engine.wait_ge(c.sem, value)

    def run(self, kind, turns, body):
        before = {c.name: c.n for c in self.counters}
        with self.nc.Fori(0, turns) as i:
            self.loop, self.waited, self.made, self.moving = (i, kind), {}, [], set()
            body(i)
        for c in self.counters:
            grown = c.n - before[c.name]
            assert grown == c.strides[kind] or (grown == 0 and c.name not in self.moving), (c.name, kind, grown)
            c.n += grown * (turns - 1)
            for mark in self.made:
                if mark.counter is c:
                    mark.value += grown * (turns - 1)
        self.loop, self.waited, self.made = None, {}, []


def build(nc, x, enc, mask_a, mask_b, mask_d, weights, columns, rows, gate, ident_in, out):
    f32, f32r, u8 = mybir.dt.float32, mybir.dt.float32r, mybir.dt.uint8
    ALU, ACT, AX = mybir.AluOpType, mybir.ActivationFunctionType, mybir.AxisListType
    pe, dve, act, pool, sp = nc.tensor, nc.vector, nc.scalar, nc.gpsimd, nc.sync
    ctx = ExitStack()
    with ctx:
        def sb(name, shape, dt=f32):
            return ctx.enter_context(nc.sbuf_tensor(name, shape, dt))

        whi = sb("weights_hi", [128, SLOTS, KC, H], f32r)
        wlo = sb("weights_lo", [128, SLOTS, KC, H], f32r)
        raw = sb("weights_raw", [128, STG, H])
        xhi = sb("inputs_hi", [128, 2, KC, GT], f32r)
        xlo = sb("inputs_lo", [128, 2, KC, GT], f32r)
        chi = sb("context_hi", [128, 2, 512], f32r)
        clo = sb("context_lo", [128, 2, 512], f32r)
        qT = sb("qT", [128, 2, KC, GT])
        kT = sb("kT", [128, 2, KC, GT])
        vv = sb("v", [128, 2, GB, H])
        prob = sb("prob", [128, 2, NH * T])
        probT = sb("probT", [128, 2, 512])
        lnx = sb("ln_tile", [128, 2, H])
        res = sb("residual", [128, 2, H])
        msk = sb("mask", [128, 2, T])
        mbias = sb("mask_bias", [128, 2, T])
        mrow = sb("mask_rows", [128, 2, T], u8)
        cols = sb("columns", [128, NCOL])
        brow = sb("bias_rows", [128, 3, H])
        ident = sb("identity", [128, 128])
        stats = sb("ln_stats", [128, 2, 6])
        mv = sb("ln_mean_var", [128, 2, 2])
        rstd = sb("ln_rstd", [128, 2])
        power = sb("minus_half", [128, 2])
        negmax = sb("negmax", [128, 2, NH])
        total = sb("total", [128, 2, NH])
        rtotal = sb("rtotal", [128, 2, NH])
        gatec = sb("gate", [128, 2])
        ps = ctx.enter_context(nc.psum_tensor("psum", [128, 8, 512], f32))
        S_BANK = 0
        T_BANK = 4
        U_BANK = 6
        xs = [x] + [nc.dram_tensor(f"stream{n}", (NB * T, H), f32, kind="Internal").ap() for n in (1, 2, 3)] + [out]

        m = Marks(nc, ctx)
        up, wait = m.up, m.wait

        c_const = m.counter("constants_loaded")
        c_power = m.counter("minus_half_set")
        c_small = m.counter("constants_made")
        c_raw = [m.counter(f"raw{k}_loaded", attention=16) for k in range(STG)]
        c_whi = m.counter("w_hi", attention=4)
        c_wlo = m.counter("w_lo", attention=4)
        c_wld = m.counter("w_lo_by_dve")
        c_lnx = [m.counter(f"ln_tile{t}_loaded", attention=32, hidden=32) for t in range(2)]
        c_rawx = [m.counter(f"raw_tile{t}_loaded", attention=32) for t in range(2)]
        c_stat = m.counter("ln_statistics", attention=8, hidden=8)
        c_rstd = m.counter("ln_rstd", attention=4, hidden=4)
        c_xhat = m.counter("normalised", attention=4, hidden=4)
        c_ft = m.counter("fill_transposed", attention=4, hidden=4)
        c_fr = m.counter("raw_fill_transposed", attention=4)
        c_y = m.counter("scaled", attention=4, hidden=4)
        c_fhi = m.counter("fill_hi", attention=4, hidden=4)
        c_flo = m.counter("fill_lo", attention=4, hidden=4)
        c_rhi = m.counter("raw_fill_hi", attention=4)
        c_rlo = m.counter("raw_fill_lo", attention=4)
        c_res = [m.counter(f"residual{t}_loaded", attention=32, hidden=32) for t in range(2)]
        c_store = [m.counter(f"residual{t}_stored", attention=32, hidden=32) for t in range(2)]
        c_resb = m.counter("residual_plus_bias", attention=4, hidden=4)
        c_mload = [m.counter(f"mask{t}_loaded", attention=32) for t in range(2)]
        c_mb = m.counter("mask_bias_made", attention=4)
        c_mb2 = m.counter("mask_bias_inf", attention=4)
        c_scores = m.counter("scores", attention=4)
        c_masked = m.counter("masked", attention=8)
        c_biased = m.counter("biased", attention=8)
        c_max = m.counter("row_max", attention=8)
        c_exp = m.counter("exps", attention=16)
        c_rt = m.counter("row_sum_inverse", attention=4)
        c_prob = m.counter("probabilities", attention=8)
        c_tr = m.counter("prob_transposed", attention=16)
        c_pta = m.counter("probT_by_act", attention=8)
        c_ptd = m.counter("probT_by_dve", attention=8)
        c_pv = m.counter("prob_times_v", attention=16)
        c_chi = m.counter("ctx_hi", attention=4)
        c_clo = m.counter("ctx_lo", attention=4)
        c_u = m.counter("projected", attention=12)
        c_ua = m.counter("qk_out", attention=8)
        c_ud = m.counter("v_out", attention=4)
        c_uv = m.counter("v_out_by_act", attention=4)
        c_o = m.counter("output_projected", attention=4)
        c_x = m.counter("stream_updated", attention=4, hidden=4)
        c_h = m.counter("hidden", hidden=16)
        c_hx = m.counter("hidden_plus_bias", hidden=16)
        c_sq = m.counter("hidden_squared", hidden=16)
        c_in = m.counter("tanh_argument", hidden=16)
        c_th = m.counter("tanh", hidden=16)
        c_gy = m.counter("gelu_twice", hidden=16)
        c_ghi = m.counter("gelu_hi", hidden=16)
        c_glo = m.counter("gelu_lo", hidden=16)
        c_w2 = m.counter("w2_applied", hidden=16)

        for c, by in [(c, 1) for c in (c_pv, c_o, c_tr, c_scores, c_exp, c_rt, c_x, c_clo, c_pta, c_ptd)] + [(c, 16) for c in c_store]:
            sp.sem_inc(c.sem, by)
            c.n += by

        bank_free = [[] for _ in range(8)]
        at = {}

        def get(key):
            return at.get(key)

        for dst, src in ((ident[:, :], ident_in), (cols[:, :], columns), (gatec[:, 0:1], gate.to_broadcast([128, 1])),
                         (msk[:, 0, :], mask_a)):
            const = up(sp.dma_start(dst, src), c_const, 16)

        def load_bias_row(name):
            return up(sp.dma_start(brow[:, ROW_SLOT[name], :], rows[ROW[name]:ROW[name] + 1, :].to_broadcast([128, H])), c_const, 16)

        pool.memset(power[:, :], -0.5).then_inc(c_power.sem, 1)
        pool.wait_ge(c_power.sem, 1)
        for name in ("A_v", "A_o", "B_o"):
            const = load_bias_row(name)

        def fixed(engine):
            if m.loop:
                engine.nop(nofuse=True)

        def load_tile(t, src, row, counter):
            wait(sp, get(("lnx free", t)))
            at["lnx", t] = up(sp.dma_start(lnx[:, t, :], src[bass.ds(row, T), :]), counter[t], 16)

        def load_weight(unit, chunk, buf):
            wait(sp, get(("raw free", buf)))
            at["raw", buf] = up(sp.dma_start(raw[:, buf, :], weights[unit, chunk, :, :]) if isinstance(unit, int)
                                else sp.dma_start(raw[:, buf, :], weights[bass.ds(unit, 1), chunk, :, :].rearrange("a p n -> (a p) n")),
                                c_raw[buf], 16)

        def split_weight(slot, chunk, buf, by=pool, counter=None):
            if isinstance(slot, int):
                dst_hi, dst_lo = whi[:, slot, chunk, :], wlo[:, slot, chunk, :]
            else:
                dst_hi, dst_lo = (w[:, bass.ds(slot, 1), chunk, :].rearrange("p a n -> p (a n)") for w in (whi, wlo))
            free = None if m.loop else get(("slot free", slot))
            wait(act, at["raw", buf], free)
            hi = up(act.activation(dst_hi, raw[:, buf, :], ACT.Copy), c_whi)
            wait(by, hi, at["raw", buf])
            at["w"] = at["w", slot if isinstance(slot, int) else "loop"] = at["raw free", buf] = up(
                by.tensor_tensor(dst_lo, raw[:, buf, :], dst_hi.bitcast(f32), ALU.subtract), counter or c_wlo)

        def statistics():
            for t in range(GB):
                wait(dve, at["lnx", t], get("xhat"))
                a = up(dve.bn_stats(stats[:, t, :], lnx[:, t, :]), c_stat)
            for t in range(GB):
                wait(dve, a)
                fixed(dve)
                b = up(dve.bn_aggr(mv[:, t, :], stats[:, t, :]), c_stat)
            wait(pool, b)
            fixed(pool)
            c = up(pool.tensor_scalar(rstd[:, :], mv[:, :, 1], EPS, None, ALU.add), c_rstd)
            wait(pool, c)
            at["rstd"] = up(pool.tensor_tensor(rstd[:, :], rstd[:, :], power[:, :], ALU.pow), c_rstd)

        def normalise():
            for t in range(GB):
                wait(dve, at["rstd"])
                at["xhat"] = at["tile", t] = up(dve.tensor_scalar(
                    lnx[:, t, :], lnx[:, t, :], mv[:, t, 0:1], rstd[:, t:t + 1], ALU.subtract, ALU.mult), c_xhat)

        def fill_transpose(t, ln):
            wait(pe, at["tile", t] if ln else at["lnx", t], *bank_free[T_BANK + t])
            for c in range(KC):
                last = pe.transpose(ps[:, T_BANK + t, 128 * c:128 * c + 128], lnx[:, t, 128 * c:128 * c + 128], ident[:, :])
            at["ft", t] = up(last, c_ft if ln else c_fr)

        def fill_split(t, ln, buf, ln_name):
            hi, lo = (v[:, buf, :, T * t:T * t + T] for v in (xhi, xlo))
            src = ps[:, T_BANK + t, :].rearrange("p (c n) -> p c n", c=KC)
            free = at.get(("inputs free", buf))
            if ln:
                y = lnx[:, t, :].rearrange("p (c n) -> p c n", c=KC)
                g0, b0 = COL[ln_name + "_s"], COL[ln_name + "_b"]
                wait(act, at["ft", t])
                for c in range(KC):
                    last = act.activation(y[:, c, :], src[:, c, :], ACT.Identity, bias=cols[:, b0 + c:b0 + c + 1],
                                          scale=cols[:, g0 + c:g0 + c + 1])
                done = up(last, c_y)
                bank_free[T_BANK + t] = [done]
                wait(dve, done, free)
                a = up(dve.tensor_copy(hi, y), c_fhi)
                wait(pool, a, free)
                b = up(pool.tensor_tensor(lo, y, hi.bitcast(f32), ALU.subtract), c_flo)
                at["lnx free", t] = b
            else:
                at["lnx free", t] = at["ft", t]
                wait(act, at["ft", t], free)
                a = up(act.activation(hi, src, ACT.Copy), c_rhi)
                wait(dve, a, free)
                b = up(dve.tensor_tensor(lo, src, hi.bitcast(f32), ALU.subtract), c_rlo)
                bank_free[T_BANK + t] = [b]
            at["inputs", buf, t] = b
            at["inputs hi", buf, t] = a

        def project(phase, name, half, g_par, buf, bank, parts=(0, 1)):
            slot = UNITS[phase][name] % SLOTS
            if 0 in parts:
                wait(pe, *[at["inputs", buf, t] for t in (range(GB) if name != "v" else [half])], *bank_free[bank])
            for part in parts:
                if name == "v":
                    tok = slice(T * half, T * half + T)
                    todo = [(c, ps[:, bank, :], a[:, buf, c, tok], w[:, slot, c, :], 3 * c + n)
                            for c in range(2 * part, 2 * part + 2) for n, (a, w) in enumerate(((xhi, whi), (xhi, wlo), (xlo, whi)))]
                else:
                    o = slice(128 * (2 * half + part), 128 * (2 * half + part) + 128)
                    todo = [(c, ps[:, bank, GT * part:GT * part + GT], w[:, slot, c, o], a[:, buf, c, :], 3 * c + n)
                            for c in range(KC) for n, (w, a) in enumerate(((whi, xhi), (whi, xlo), (wlo, xhi)))]
                for c, dst, stationary, moving, n in todo:
                    last = pe.matmul(dst, stationary, moving, start=n == 0, stop=n == 3 * KC - 1)
            if 1 not in parts:
                return
            done = up(last, c_u)
            at["inputs free", buf] = at["slot free", slot] = done
            if name == "v":
                old = get(("v free", g_par))
                if phase == "D":
                    wait(act, done, old)
                    e = up(act.activation(vv[:, g_par, half, :], ps[:, bank, :], ACT.Copy), c_uv)
                else:
                    wait(dve, done, old)
                    e = up(dve.tensor_tensor(vv[:, g_par, half, :], ps[:, bank, :], brow[:, ROW_SLOT[phase + "_v"], :], ALU.add), c_ud)
            else:
                dst = (qT if name == "q" else kT)[:, g_par, 2 * half:2 * half + 2, :]
                wait(act, done, get(("qk free", g_par)))
                if phase == "D":
                    e = up(act.activation(dst, ps[:, bank, :].rearrange("p (c n) -> p c n", c=2), ACT.Copy), c_ua)
                else:
                    col = COL[f"{phase}_{name}"] + 2 * half
                    for k in range(2):
                        last = act.activation(dst[:, k, :], ps[:, bank, GT * k:GT * k + GT], ACT.Identity,
                                              bias=cols[:, col + k:col + k + 1])
                    e = up(last, c_ua)
            at[name, g_par] = e
            bank_free[bank] = [e]

        def unit_list(phase):
            if phase == "A":
                return [("q", 0, None), ("q", 1, None), ("k", 0, None), ("k", 1, None), ("v", 0, None), ("v", 1, None)]
            return [("k", 0, 0), ("k", 1, 0), ("v", 0, 0), ("v", 1, 0), ("q", 0, 1), ("q", 1, 1)]

        def mask_bias(phase, b, par):
            if phase == "B":
                wait(dve, at["mask", par], get(("mask bias free", par)))
                at["mask bias", par] = up(dve.tensor_scalar(mbias[:, par, :], msk[:, par, :], 1.0, 10000.0, ALU.subtract, ALU.mult), c_mb)
            if phase == "D":
                row = mrow[:, par, :]
                wait(dve, at["mask", par], get(("mask bias free", par)))
                a = at["mask free", par] = up(dve.tensor_scalar(mbias[:, par, :], row, 1.0, 3e38, ALU.subtract, ALU.mult), c_mb)
                wait(dve, a)
                at["mask bias", par] = up(dve.tensor_scalar(mbias[:, par, :], mbias[:, par, :], 4.0, None, ALU.mult), c_mb2)

        def period(phase, b, k, prev, cur=True, units=None, fills=(), weight=None, extra=()):
            par, gp, half = k % 2, (k // 2) % 2, k % 2
            pp = 1 - par
            pgp, phalf = ((k - 1) // 2) % 2, (k - 1) % 2
            P, Pp = prob[:, par, :], prob[:, pp, :]
            heads = lambda v: v.rearrange("p (h n) -> p h n", n=T)

            if prev:
                pph, pb = prev
                wait(sp, get(("stored", pp)))
                at["res", pp] = up(sp.dma_start(res[:, pp, :], xs["ABCD".index(pph)][bass.ds(pb * T, T), :]), c_res[pp], 16)
            for t in range(GB if fills else 0):
                src, row, ln_name, buf = fills
                load_tile(t, src, row + t * T, c_lnx if ln_name else c_rawx)
            if weight:
                load_weight(weight[0], weight[2], k % STG)
            if cur:
                wait(pe, at["q", gp], at["k", gp], at["v", gp], *(f for j in range(4) for f in bank_free[j]))
                for c in range(KC):
                    for j in range(4):
                        r, tk = slice(32 * j, 32 * j + 32), slice(T * half, T * half + T)
                        last = pe.matmul(ps[:, S_BANK + j, T * c:T * c + T], qT[r, gp, c, tk], kT[r, gp, c, tk], start=True, stop=True)
                scores = up(last, c_scores)
                if half == 1:
                    at["qk free", gp] = scores
                mask_bias(phase, b, par)
                Sps = ps[:, 0:4, :].rearrange("p a n -> p (a n)")
                for h in range(2):
                    s = slice(1024 * h, 1024 * h + 1024)
                    wait(dve, scores, at["mask bias", par if phase != "A" else 0], get(("prob free", par)), const)
                    other = (msk[:, par if phase == "B" else 0, :] if phase != "D" else mbias[:, par, :])
                    at["masked", h] = up(dve.scalar_tensor_tensor(
                        heads(P[:, s]), heads(Sps[:, s]), SCALE, other.unsqueeze(1).to_broadcast([128, 8, T]),
                        ALU.mult, ALU.add if phase == "D" else ALU.mult), c_masked)
                    bank_free[2 * h] = bank_free[2 * h + 1] = [at["masked", h]]
                if phase == "D":
                    at["mask bias free", par] = at["masked", 1]
                if phase != "D":
                    at["mask free", par if phase == "B" else 0] = at["masked", 1]
                if phase != "D":
                    for h in range(2):
                        s = slice(1024 * h, 1024 * h + 1024)
                        wait(pool, at["masked", h], at["mask bias", par if phase == "B" else 0])
                        mb = mbias[:, par if phase == "B" else 0, :]
                        at["masked", h] = up(pool.tensor_tensor(heads(P[:, s]), heads(P[:, s]),
                                                                mb.unsqueeze(1).to_broadcast([128, 8, T]), ALU.add), c_biased)
                    at["mask bias free", par if phase == "B" else 0] = at["masked", 1]

            if cur and phase != "A" and not (isinstance(b, int) and b == NB - 1):
                load_mask(phase, b, k)

            def row_max(h):
                wait(dve, at["masked", h], get(("max free", par)))
                at["max", h] = up(dve.tensor_reduce(negmax[:, par, 8 * h:8 * h + 8], heads(P[:, 1024 * h:1024 * h + 1024]),
                                                    AX.X, ALU.max, negate=True), c_max)

            def exps(q):
                wait(act, at["max", q // 2], at["masked", q // 2], get(("total free", par)))
                for s in range(4 * q, 4 * q + 4):
                    last = act.activation(P[:, T * s:T * s + T], P[:, T * s:T * s + T], ACT.Exp,
                                          bias=negmax[:, par, s:s + 1], accum_out=total[:, par, s:s + 1])
                at["exp"] = up(last, c_exp)

            def unit(n, bank, parts=(0, 1)):
                if units:
                    uph, lst, ugp = units
                    name, hf, buf = lst[n]
                    project(uph, name, hf, ugp, ugp if buf is None else buf, bank, parts)

            def transpose_prob(c):
                bank = T_BANK + c % 2
                wait(pe, at["prob", pp], *bank_free[bank])
                for j in range(4):
                    last = pe.transpose(ps[:, bank, T * j:T * j + T], Pp[:, T * (4 * j + c):T * (4 * j + c) + T], ident[:, :])
                done = up(last, c_tr)
                if c == KC - 1:
                    at["prob free", pp] = done
                if c % 2 == 0:
                    wait(act, done, get(("probT free", 0)))
                    e = up(act.activation(probT[:, 0, :], ps[:, bank, :], ACT.Copy), c_pta)
                else:
                    wait(dve, done, get(("probT free", 1)))
                    e = up(dve.tensor_copy(probT[:, 1, :], ps[:, bank, :]), c_ptd)
                bank_free[bank] = [e]
                at["probT", c % 2] = e

            def times_v(c):
                wait(pe, at["probT", c % 2], *(bank_free[0] if c == 0 else []))
                for j in range(4):
                    o = (4 * c + j) * HD
                    last = pe.matmul(ps[32 * j:32 * j + 32, 0, T * c:T * c + T], vv[:, pgp, phalf, o:o + HD],
                                     probT[:, c % 2, T * j:T * j + T], start=True, stop=True)
                at["pv"] = at["probT free", c % 2] = up(last, c_pv)
                if c == KC - 1 and phalf == 1:
                    at["v free", pgp] = at["pv"]

            def context_split():
                wait(act, at["pv"], get("ctx free"))
                a = up(act.activation(chi[:, 0, :], ps[:, 0, :], ACT.Copy), c_chi)
                wait(dve, a, get("ctx free"))
                at["ctx"] = up(dve.tensor_tensor(clo[:, 0, :], ps[:, 0, :], chi[:, 0, :].bitcast(f32), ALU.subtract), c_clo)
                bank_free[0] = [at["ctx"]]

            normal = bool(fills) and fills[2] is not None
            unit(0, U_BANK)
            if normal:
                statistics()
            if prev:
                transpose_prob(0)
                transpose_prob(1)
            if cur:
                row_max(0)
                exps(0)
            unit(1, U_BANK + 1)
            if cur:
                row_max(1)
            if prev:
                times_v(0)
                times_v(1)
                transpose_prob(2)
                transpose_prob(3)
            if normal:
                normalise()
            if cur:
                exps(1)
            unit(2, U_BANK, parts=(0,))
            if prev:
                times_v(2)
                times_v(3)
                context_split()
            unit(2, U_BANK, parts=(1,))
            if cur:
                exps(2)
            for t in range(GB if fills else 0):
                fill_transpose(t, normal)
                fill_split(t, normal, fills[3], fills[2])
            if cur:
                exps(3)
            if prev:
                slot = UNITS[pph]["o"] % SLOTS
                if pph != "D":
                    wait(pool, at["res", pp], const)
                    resb = up(pool.tensor_tensor(res[:, pp, :], res[:, pp, :], brow[:, ROW_SLOT[pph + "_o"], :], ALU.add), c_resb)
                wait(pe, at["ctx"], *bank_free[U_BANK + 1])
                n = 0
                for c in range(KC):
                    cs = slice(T * c, T * c + T)
                    for a, w in ((chi, whi), (chi, wlo), (clo, whi)):
                        last = pe.matmul(ps[:, U_BANK + 1, :], a[:, 0, cs], w[:, slot, c, :], start=n == 0, stop=n == 3 * KC - 1)
                        n += 1
                done = at["ctx free"] = at["slot free", slot] = up(last, c_o)
                if pph != "D":
                    wait(dve, done, resb)
                    e = up(dve.tensor_tensor(res[:, pp, :], ps[:, U_BANK + 1, :], res[:, pp, :], ALU.add), c_x)
                else:
                    wait(dve, done, at["res", pp])
                    e = up(dve.scalar_tensor_tensor(res[:, pp, :], ps[:, U_BANK + 1, :], gatec[:, 1:2], res[:, pp, :],
                                                    ALU.mult, ALU.add), c_x)
                bank_free[U_BANK + 1] = [e]
                wait(sp, e)
                at["stored", pp] = up(sp.dma_start(xs["ABCD".index(pph) + 1][bass.ds(pb * T, T), :], res[:, pp, :]), c_store[pp], 16)
            if cur:
                wait(dve, at["exp"])
                r = up(dve.reciprocal(rtotal[:, par, :], total[:, par, :]), c_rt)
                at["total free", par] = r
                at["max free", par] = at["exp"]
                wait(dve, r)
                for h in range(2):
                    s = slice(1024 * h, 1024 * h + 1024)
                    rb = rtotal[:, par, 8 * h:8 * h + 8].unsqueeze(2).to_broadcast([128, 8, T])
                    at["prob", par] = up(dve.tensor_tensor(heads(P[:, s]), heads(P[:, s]), rb, ALU.mult), c_prob)
            if weight:
                split_weight(weight[1], weight[2], k % STG)
            for f in extra:
                f()

        def load_mask(phase, b, k):
            p, row = (k + 1) % 2, bass.ds((b + 1) * T, T)
            wait(sp, get(("mask free", p)))
            if phase == "B":
                ins = sp.dma_start(msk[:, p, :], mask_b[row, :])
            else:
                ins = sp.dma_start(mrow[:, p, :], mask_d[:, row].to_broadcast([128, T]))
            at["mask", p] = up(ins, c_mload[p], 16)

        def weight_now(units, chunks=range(KC)):
            todo = [(u, c) for u in units for c in chunks]
            for n, (u, c) in enumerate(todo):
                load_weight(u, c, n % STG)
                split_weight(u % SLOTS, c, n % STG)

        def attention(phase, first_prev, last_units, kv, q, next_kv, weights_from, weights_after, last_fills):
            lst = unit_list(phase)

            def step(b, k, i=None):
                odd = k % 2
                gp_next = (k // 2 + 1) % 2
                fills = ()
                if odd:
                    buf = (k // 2) % 2 if phase == "A" else 0
                    fills = (kv[0], (b - 1 + 2 * GB) * T, kv[1], buf)
                elif phase != "A":
                    fills = (q[0], (b + GB) * T, q[1], 1)
                weight = None
                if weights_from is not None:
                    u = b // 4 if i is None else i + (k == 0)
                    weight = (u + weights_from, u + weights_from % SLOTS, k)
                return dict(units=(phase, lst[3 * odd:3 * odd + 3], gp_next), fills=fills, weight=weight)

            if first_prev is None:
                pv, o, tr, sc, ex, rt = m.now(c_pv, c_o, c_tr, c_scores, c_exp, c_rt)
                at.update({("probT free", 0): pv, ("probT free", 1): pv, "ctx free": o, ("prob free", 1): tr,
                           ("v free", 1): pv, ("qk free", 1): sc, ("max free", 1): ex, ("total free", 1): rt})
                at["stored", 0], at["stored", 1] = m.now(*c_store)
                finished = {U_BANK + 1: m.now(c_x), 0: m.now(c_clo), T_BANK: m.now(c_pta), T_BANK + 1: m.now(c_ptd)}
            if phase == "B":
                at["mask free", 1], at["mask bias free", 1] = m.now(c_masked, c_biased)
            if phase == "D":
                at["mask bias free", 1], = m.now(c_masked)
                at["mask free", 1], = m.now(c_mb)
                load_mask("D", -1, 3)

            period(phase, 0, 0, first_prev, **step(0, 0))
            if first_prev is None:
                for bank, marks in finished.items():
                    bank_free[bank] = bank_free[bank] + marks
            if weights_from is not None:
                for slot in range(weights_from % SLOTS, weights_from % SLOTS + 4):
                    wait(act, get(("slot free", slot)))
                    wait(pool, get(("slot free", slot)))

            def body(i):
                for k in (1, 2, 3, 4):
                    b = i * 4 + k
                    period(phase, b, k % 4, (phase, i * 4 + (k - 1)), **step(b, k % 4, i))

            m.run("attention", 3, body)
            kw = step(13, 1)
            kw["fills"] = next_kv
            period(phase, 13, 1, (phase, 12), **kw)
            if phase == "A":
                wait(sp, *m.now(c_ud))
                b_v = load_bias_row("B_v")
                wait(dve, b_v)
            for b in (14, 15):
                kw = step(b, b % 4)
                kw["units"], kw["fills"] = None, last_fills[b - 14]
                if last_units:
                    wait(pe, at["w"])
                    kw["units"] = (last_units, unit_list(last_units)[3 * (b - 14):3 * (b - 14) + 3], 0)
                if weights_after:
                    kw["extra"] = [lambda u=weights_after[b - 14]: weight_now([u])]
                period(phase, b, b % 4, (phase, b - 1), **kw)
            wait(pe, at["w"])

        hx = lambda n: prob[:, 0, 512 * (n % 4):512 * (n % 4) + 512]
        hw = lambda n: prob[:, 1, 512 * (n % 4):512 * (n % 4) + 512]

        def pair(g, gp, jp, cur=True, ahead=1, last=2):
            bank = U_BANK + jp % 2
            if cur:
                slot = W1_UNIT[jp // 2] % SLOTS
                wait(pe, at["inputs", gp, 0], at["inputs", gp, 1], *bank_free[bank], None if m.loop else get(("w", slot)))
                for e in range(2):
                    o = slice(128 * (2 * (jp % 2) + e), 128 * (2 * (jp % 2) + e) + 128)
                    n = 0
                    for c in range(KC):
                        for w, a in ((whi, xhi), (whi, xlo), (wlo, xhi)):
                            mm = pe.matmul(ps[:, bank, GT * e:GT * e + GT], w[:, slot, c, o], a[:, gp, c, :],
                                           start=n == 0, stop=n == 3 * KC - 1)
                            n += 1
                h = at["slot free", slot] = at["inputs free", gp] = up(mm, c_h)
            if ahead:
                q = (jp - 1) % 4
                wait(act, at["tanh in", q])
                th = up(act.activation(hw(q), hw(q), ACT.Tanh, scale=GELU_A * GELU_C), c_th)
            if cur:
                wait(act, h, get(("hx free", jp % 4)))
                for e in range(2):
                    col = COL["b1"] + 2 * jp + e
                    ins = act.activation(hx(jp)[:, GT * e:GT * e + GT], ps[:, bank, GT * e:GT * e + GT], ACT.Identity,
                                         bias=cols[:, col:col + 1])
                x_ = up(ins, c_hx)
                bank_free[bank] = [x_]
                wait(act, x_, get(("hw free", jp % 4)))
                sq = up(act.activation(hw(jp), hx(jp), ACT.Square), c_sq)
            if ahead:
                wait(dve, th, at["hx", q])
                y = up(dve.scalar_tensor_tensor(hw(q), hw(q), 1.0, hx(q), ALU.add, ALU.mult), c_gy)
                at["hx free", q] = y
                gb = (jp - 1) % 2
                wait(dve, y, get(("gelu free", gb)))
                ghi = up(dve.tensor_scalar(chi[:, gb, :], hw(q), 0.5, None, ALU.mult), c_ghi)
            if cur:
                wait(dve, sq, x_)
                at["tanh in", jp % 4] = up(dve.scalar_tensor_tensor(hw(jp), hw(jp), 1.0 / GELU_A, hx(jp), ALU.add, ALU.mult), c_in)
                at["hx", jp % 4] = x_
            if ahead:
                wait(dve, ghi, get(("gelu free", gb)))
                at["gelu", gb] = at["hw free", q] = up(dve.scalar_tensor_tensor(
                    clo[:, gb, :], hw(q), 0.5, chi[:, gb, :].bitcast(f32), ALU.mult, ALU.subtract), c_glo)
            if last:
                j2, g2 = (jp - 2) % NPAIR, gp if jp >= 2 else 1 - gp
                slot, gb = W2_UNIT[j2 // 2] % SLOTS, jp % 2
                for t in range(GB):
                    acc = 2 * g2 + t
                    wait(pe, at["gelu ready", gb], *(bank_free[acc] if j2 == 0 else []), None if m.loop else get(("w", slot)))
                    n = 0
                    for e in range(2):
                        tok = slice(GT * e + T * t, GT * e + T * t + T)
                        for a, w in ((chi, whi), (chi, wlo), (clo, whi)):
                            mm = pe.matmul(ps[:, acc, :], a[:, gb, tok], w[:, slot, 2 * (j2 % 2) + e, :],
                                           start=j2 == 0 and n == 0, stop=j2 == NPAIR - 1 and n == 5)
                            n += 1
                at["gelu free", gb] = at["slot free", slot] = up(mm, c_w2)
            if ahead:
                at["gelu ready", (jp - 1) % 2] = at["gelu", (jp - 1) % 2]

        def mlp_out(g, g2):
            done = at["gelu free", 1]
            for t in range(GB):
                wait(pool, at["res", t])
                rb = up(pool.tensor_tensor(res[:, t, :], res[:, t, :], brow[:, ROW_SLOT["C_o"], :], ALU.add), c_resb)
                wait(dve, done, rb)
                e = up(dve.tensor_tensor(res[:, t, :], ps[:, 2 * g2 + t, :], res[:, t, :], ALU.add), c_x)
                bank_free[2 * g2 + t] = [e]
                wait(sp, e)
                at["stored", t] = up(sp.dma_start(xs[3][bass.ds(g * GT + t * T, T), :], res[:, t, :]), c_store[t], 16)

        def mlp_residual(g):
            for t in range(GB):
                wait(sp, at["stored", t])
                at["res", t] = up(sp.dma_start(res[:, t, :], xs[2][bass.ds(g * GT + t * T, T), :]), c_res[t], 16)

        def group(g, gp, fills, first=False, weights=None):
            for jp in range(NPAIR):
                if jp == 0 and not first:
                    mlp_residual(g - 1)
                if jp == 0:
                    src, row, ln_name, buf = fills
                    for t in range(GB):
                        load_tile(t, src, row + t * T, c_lnx)
                pair(g, gp, jp, ahead=not (first and jp == 0), last=not (first and jp < 2))
                if jp == 1 and not first:
                    mlp_out(g - 1, 1 - gp)
                if jp == 2:
                    statistics()
                if jp == 3:
                    normalise()
                if jp == 4:
                    for t in range(GB):
                        fill_transpose(t, True)
                        fill_split(t, True, buf, ln_name)
                if weights and jp in weights:
                    weight_now([weights[jp]])

        for t in range(GB):
            load_tile(t, x, t * T, c_lnx)
        wait(dve, const)
        at["mask bias", 0] = up(dve.tensor_scalar(mbias[:, 0, :], msk[:, 0, :], 1.0, 10000.0, ALU.subtract, ALU.mult), c_small)
        wait(act, const)
        tanh = up(act.activation(gatec[:, 1:2], gatec[:, 0:1], ACT.Tanh), c_small)
        wait(dve, tanh)
        wait(pe, const)
        def weight_start(unit):
            for c in range(KC):
                load_weight(unit, c, c)
            for c in range(KC):
                split_weight(unit % SLOTS, c, c, by=dve, counter=c_wld)

        weight_start(0)
        for g in range(2):
            if g:
                for t in range(GB):
                    load_tile(t, x, (GB * g + t) * T, c_lnx)
            statistics()
            normalise()
            for t in range(GB):
                fill_transpose(t, True)
                fill_split(t, True, g, "ln1")
            if g == 0:
                weight_start(1)
                weight_start(2)
        for n, (name, hf, _) in enumerate(unit_list("A")):
            wait(pe, at["w", UNITS["A"][name]])
            project("A", name, hf, 0, 0, U_BANK + n % 2)
        weight_start(3)
        wait(pe, at["w"])

        attention("A", None, "B", (x, "ln1"), None, (enc, 0, None, 0), 4, None,
                  [(xs[1], 0, "ln2", 1), (enc, GT, None, 0)])
        load_mask("B", -1, 3)
        attention("B", ("A", NB - 1), None, (enc, None), (xs[1], "ln2"), (xs[2], 0, "ln3", 0), 8, [12, 13],
                  [(), ()])
        period("B", NB, 0, ("B", NB - 1), cur=False)
        weight_now([14, 15])
        wait(sp, *m.now(c_resb))
        wait(pool, load_bias_row("C_o"))

        group(0, 0, (xs[2], GT, "ln3", 1), first=True)
        at["stored", 0], at["stored", 1] = m.now(*c_store)

        def body(i):
            for k in (1, 2):
                group(i * 2 + k, k % 2, (xs[2], (i * 2 + (k + 1)) * GT, "ln3", (k + 1) % 2))

        m.run("hidden", 3, body)
        group(NG - 1, 1, (enc, 0, "lna", 0), weights={3: 16, 4: 17, 5: 18, 7: 19})
        mlp_residual(NG - 1)
        for t in range(GB):
            load_tile(t, xs[3], t * T, c_rawx)
        pair(NG, 0, 0, cur=False)
        pair(NG, 0, 1, cur=False, ahead=False)
        mlp_out(NG - 1, 1)

        for t in range(GB):
            fill_transpose(t, False)
            fill_split(t, False, 1, None)
        for n, (name, hf, buf) in enumerate(unit_list("D")):
            wait(pe, at["w", UNITS["D"][name] % SLOTS])
            project("D", name, hf, 0, buf, U_BANK + n % 2)
        for t in range(GB):
            load_tile(t, enc, GT + t * T, c_lnx)
        statistics()
        normalise()
        for t in range(GB):
            fill_transpose(t, True)
            fill_split(t, True, 0, "lna")
        wait(pe, at["w"])
        attention("D", None, None, (enc, "lna"), (xs[3], None), (), None, None, [(), ()])
        period("D", NB, 0, ("D", NB - 1), cur=False)
        for p in range(2):
            wait(sp, at["stored", p])


def kernel(x, ctx_2048, mask_1x1xSxS2_fc1, mask_Bx1xSxS2_ff1, mask_BxS2_bf1, **p):
    import numpy as np
    import concourse.bacc as bacc
    from concourse.bass_utils import run_bass_kernel_spmd

    a = {k.removeprefix("L0_xattn_").replace("L1_xattn_", "L1_"): np.asarray(v) for k, v in p.items()}

    def unit(w, r, c):
        return w[H * r:H * r + H, H * c:H * c + H].reshape(KC, 128, H)

    blocks = [unit(a["w_qkv"], 0, 0), unit(a["w_qkv"], 0, 1), unit(a["w_qkv"], 0, 2), unit(a["w_ao"], 0, 0),
              unit(a["w_q"], 0, 0), unit(a["w_kv"], 0, 0), unit(a["w_kv"], 0, 1), unit(a["w_co"], 0, 0)]
    for j in range(4):
        blocks += [unit(a["w1"], 0, j), unit(a["w2"], j, 0)]
    blocks += [unit(a[f"L1_W{n}"].T, 0, 0) for n in "kvqo"]
    b_qkv, b_kv = a["b_qkv"], a["b_kv"]
    columns = np.concatenate([v.reshape(-1, 128).T for v in (
        a["ln1_s"], a["ln1_b"], a["ln2_s"], a["ln2_b"], a["ln3_s"], a["ln3_b"], a["L1_ln_gamma"], a["L1_ln_beta"],
        b_qkv[:H], b_qkv[H:2 * H], a["b_q"], b_kv[:H], a["b1"])], axis=1)
    rows = np.stack([b_qkv[2 * H:], a["b_ao"], b_kv[H:], a["b_co"], a["b2"]])
    arrays = dict(
        x=np.asarray(x).reshape(NB * T, H), enc=np.asarray(ctx_2048).reshape(NB * T, H),
        mask_a=np.asarray(mask_1x1xSxS2_fc1).reshape(T, T), mask_b=np.asarray(mask_Bx1xSxS2_ff1).reshape(NB * T, T),
        mask_d=np.asarray(mask_BxS2_bf1).reshape(1, NB * T).view(np.uint8),
        weights=np.stack(blocks), columns=columns, rows=rows, gate=a["L1_gate"].reshape(1, 1),
        ident=np.eye(128, dtype=np.float32))
    nc = bacc.Bacc("TRN2", target_bir_lowering=False, num_devices=1, dynamic_dma_scratch_size=1024)
    arrays = {f"{k}_in": np.ascontiguousarray(v) for k, v in arrays.items()}
    args = [nc.dram_tensor(k, v.shape, mybir.dt.from_np(v.dtype), kind="ExternalInput").ap() for k, v in arrays.items()]
    args.append(nc.dram_tensor("result", (NB * T, H), mybir.dt.float32, kind="ExternalOutput").ap())
    build(nc, *args)
    r = run_bass_kernel_spmd(nc, [arrays], core_ids=[0])
    return r.results[0]["result"].reshape(NB, T, H)
```

```python
from contextlib import ExitStack

import concourse.bass as bass
from concourse import mybir

NB, T, H = 16, 128, 512
NH, HD = 16, 32
KC = H // 128
GB = 2
GT = GB * T
NG = NB // GB
FF = 4 * H
NPAIR = FF // 256
SLOTS = 8
STG = 4
FIRST, SECOND, OUT = "first half", "second half", "out of PSUM"
EPS = 1e-5
SCALE = float(HD) ** -0.5
GELU_A, GELU_C = 0.044715, 0.7978845608028654

UNITS = {"A": dict(q=0, k=1, v=2, o=3), "B": dict(q=4, k=5, v=6, o=7), "D": dict(k=16, v=17, q=18, o=19)}
W1_UNIT = [8, 10, 12, 14]
W2_UNIT = [9, 11, 13, 15]
COL = dict(ln1_s=0, ln1_b=4, ln2_s=8, ln2_b=12, ln3_s=16, ln3_b=20, lna_s=24, lna_b=28,
           A_q=32, A_k=36, B_q=40, B_k=44, b1=48)
NCOL = 48 + FF // 128
ROW = dict(A_v=0, A_o=1, B_v=2, B_o=3, C_o=4)
ROW_SLOT = dict(A_v=0, A_o=1, B_v=0, B_o=2, C_o=1)


class Mark:

    def __init__(self, counter, value):
        self.counter, self.value = counter, value


class Counter:

    def __init__(self, sem, strides):
        self.sem, self.n, self.strides = sem, 0, strides


class Marks:

    def __init__(self, nc, ctx):
        self.nc, self.ctx = nc, ctx
        self.counters, self.made = [], []
        self.loop = None
        self.waited = {}

    def counter(self, name, attention=0, hidden=0):
        c = Counter(self.ctx.enter_context(self.nc.semaphore(name)), dict(attention=attention, hidden=hidden))
        c.name = name
        self.counters.append(c)
        return c

    def now(self, *counters):
        return [Mark(c, c.n) for c in counters]

    def up(self, instruction, counter, by=1):
        instruction.then_inc(counter.sem, by)
        counter.n += by
        mark = Mark(counter, counter.n)
        if self.loop:
            self.made.append(mark)
        return mark

    def wait(self, engine, *marks):
        for mark in marks:
            if mark is None:
                continue
            c = mark.counter
            key = (engine.engine, c.name)
            if self.waited.get(key, 0) >= mark.value:
                continue
            self.waited[key] = mark.value
            value = mark.value
            if self.loop and c.strides[self.loop[1]]:
                self.moving.add(c.name)
                assert mark.value > 0, c.name
                value = self.loop[0] * c.strides[self.loop[1]] + value
            engine.wait_ge(c.sem, value)

    def run(self, kind, turns, body):
        before = {c.name: c.n for c in self.counters}
        with self.nc.Fori(0, turns) as i:
            self.loop, self.waited, self.made, self.moving = (i, kind), {}, [], set()
            body(i)
        for c in self.counters:
            grown = c.n - before[c.name]
            assert grown == c.strides[kind] or (grown == 0 and c.name not in self.moving), (c.name, kind, grown)
            c.n += grown * (turns - 1)
            for mark in self.made:
                if mark.counter is c:
                    mark.value += grown * (turns - 1)
        self.loop, self.waited, self.made = None, {}, []


def build(nc, x, enc, mask_a, mask_b, mask_d, weights, columns, rows, gate, ident_in, out):
    f32, f32r, u8 = mybir.dt.float32, mybir.dt.float32r, mybir.dt.uint8
    ALU, ACT, AX = mybir.AluOpType, mybir.ActivationFunctionType, mybir.AxisListType
    pe, dve, act, pool, sp = nc.tensor, nc.vector, nc.scalar, nc.gpsimd, nc.sync
    ctx = ExitStack()
    with ctx:
        def sb(name, shape, dt=f32):
            return ctx.enter_context(nc.sbuf_tensor(name, shape, dt))

        whi = sb("weights_hi", [128, SLOTS, KC, H], f32r)
        wlo = sb("weights_lo", [128, SLOTS, KC, H], f32r)
        raw = sb("weights_raw", [128, STG, H])
        xhi = sb("inputs_hi", [128, 2, KC, GT], f32r)
        xlo = sb("inputs_lo", [128, 2, KC, GT], f32r)
        chi = sb("context_hi", [128, 2, 512], f32r)
        clo = sb("context_lo", [128, 2, 512], f32r)
        qT = sb("qT", [128, 2, KC, GT])
        kT = sb("kT", [128, 2, KC, GT])
        vv = sb("v", [128, 2, GB, H])
        prob = sb("prob", [128, 2, NH * T])
        probT = sb("probT", [128, 2, 512])
        lnx = sb("ln_tile", [128, 2, H])
        res = sb("residual", [128, 2, H])
        msk = sb("mask", [128, 2, T])
        mbias = sb("mask_bias", [128, 2, T])
        mrow = sb("mask_rows", [128, 2, T], u8)
        cols = sb("columns", [128, NCOL])
        brow = sb("bias_rows", [128, 3, H])
        ident = sb("identity", [128, 128])
        stats = sb("ln_stats", [128, 2, 6])
        mv = sb("ln_mean_var", [128, 2, 2])
        rstd = sb("ln_rstd", [128, 2])
        power = sb("minus_half", [128, 2])
        negmax = sb("negmax", [128, 2, NH])
        total = sb("total", [128, 2, NH])
        rtotal = sb("rtotal", [128, 2, NH])
        gatec = sb("gate", [128, 2])
        ps = ctx.enter_context(nc.psum_tensor("psum", [128, 8, 512], f32))
        S_BANK = 0
        T_BANK = 4
        U_BANK = 6
        xs = [x] + [nc.dram_tensor(f"stream{n}", (NB * T, H), f32, kind="Internal").ap() for n in (1, 2, 3)] + [out]

        m = Marks(nc, ctx)
        up, wait = m.up, m.wait

        c_first = m.counter("identity_and_columns_loaded")
        c_const = m.counter("constants_loaded")
        c_start = [m.counter(f"unit{u}_of_start_loaded") for u in (1, 2)]
        c_power = m.counter("minus_half_set")
        c_small = m.counter("constants_made")
        c_raw = [m.counter(f"raw{k}_loaded", attention=16) for k in range(STG)]
        c_whi = m.counter("w_hi", attention=4)
        c_wlo = m.counter("w_lo", attention=4)
        c_wld = m.counter("w_lo_by_dve")
        c_lnx = [m.counter(f"ln_tile{t}_loaded", attention=32, hidden=32) for t in range(2)]
        c_rawx = [m.counter(f"raw_tile{t}_loaded", attention=32) for t in range(2)]
        c_stat = m.counter("ln_statistics", attention=8, hidden=8)
        c_rstd = m.counter("ln_rstd", attention=4, hidden=4)
        c_xhat = m.counter("normalised", attention=4, hidden=4)
        c_ft = m.counter("fill_transposed", attention=4, hidden=4)
        c_fr = m.counter("raw_fill_transposed", attention=4)
        c_y = m.counter("scaled", attention=4, hidden=4)
        c_fhi = m.counter("fill_hi", attention=4, hidden=4)
        c_flo = m.counter("fill_lo", attention=4, hidden=4)
        c_rhi = m.counter("raw_fill_hi", attention=4)
        c_rlo = m.counter("raw_fill_lo", attention=4)
        c_res = [m.counter(f"residual{t}_loaded", attention=32, hidden=32) for t in range(2)]
        c_store = [m.counter(f"residual{t}_stored", attention=32, hidden=32) for t in range(2)]
        c_resb = m.counter("residual_plus_bias", attention=4, hidden=4)
        c_mload = [m.counter(f"mask{t}_loaded", attention=32) for t in range(2)]
        c_mb = m.counter("mask_bias_made", attention=4)
        c_mb2 = m.counter("mask_bias_inf", attention=4)
        c_scores = m.counter("scores", attention=4)
        c_masked = m.counter("masked", attention=8)
        c_biased = m.counter("biased", attention=8)
        c_max = m.counter("row_max", attention=8)
        c_exp = m.counter("exps", attention=16)
        c_rt = m.counter("row_sum_inverse", attention=8)
        c_prob = m.counter("probabilities", attention=8)
        c_tr = m.counter("prob_transposed", attention=16)
        c_pta = m.counter("probT_by_act", attention=8)
        c_ptd = m.counter("probT_by_dve", attention=8)
        c_pv = m.counter("prob_times_v", attention=16)
        c_chi = m.counter("ctx_hi", attention=4)
        c_clo = m.counter("ctx_lo", attention=4)
        c_u = m.counter("projected", attention=12)
        c_ua = m.counter("qk_out", attention=8)
        c_ud = m.counter("v_out", attention=4)
        c_uv = m.counter("v_out_by_act", attention=4)
        c_o = m.counter("output_projected", attention=4)
        c_x = m.counter("stream_updated", attention=4, hidden=4)
        c_h = m.counter("hidden", hidden=16)
        c_hx = m.counter("hidden_plus_bias", hidden=16)
        c_sq = m.counter("hidden_squared", hidden=16)
        c_in = m.counter("tanh_argument", hidden=16)
        c_th = m.counter("tanh", hidden=16)
        c_gy = m.counter("gelu_twice", hidden=16)
        c_ghi = m.counter("gelu_hi", hidden=16)
        c_glo = m.counter("gelu_lo", hidden=16)
        c_w2 = m.counter("w2_applied", hidden=16)

        for c, by in [(c, 1) for c in (c_pv, c_o, c_tr, c_scores, c_exp, c_rt, c_x, c_clo, c_pta, c_ptd)] + [(c, 16) for c in c_store]:
            sp.sem_inc(c.sem, by)
            c.n += by

        bank_free = [[] for _ in range(8)]
        at = {}

        def get(key):
            return at.get(key)

        def load_bias_row(name):
            return up(sp.dma_start(brow[:, ROW_SLOT[name], :], rows[ROW[name]:ROW[name] + 1, :].to_broadcast([128, H])), c_const, 16)

        pool.memset(power[:, :], -0.5).then_inc(c_power.sem, 1)
        pool.wait_ge(c_power.sem, 1)
        act.wait_ge(c_power.sem, 1)
        table = up(act.activation(gatec[:, 1:2], power[:, 0:1], ACT.Tanh), c_small)

        def fixed(engine):
            if m.loop:
                engine.nop(nofuse=True)

        def load_tile(t, src, row, counter):
            wait(sp, get(("lnx free", t)))
            at["lnx", t] = up(sp.dma_start(lnx[:, t, :], src[bass.ds(row, T), :]), counter[t], 16)

        def load_weight(unit, chunk, buf):
            wait(sp, get(("raw free", buf)))
            at["raw", buf] = up(sp.dma_start(raw[:, buf, :], weights[unit, chunk, :, :]) if isinstance(unit, int)
                                else sp.dma_start(raw[:, buf, :], weights[bass.ds(unit, 1), chunk, :, :].rearrange("a p n -> (a p) n")),
                                c_raw[buf], 16)

        def split_weight(slot, chunk, buf, by=pool, counter=None):
            if isinstance(slot, int):
                dst_hi, dst_lo = whi[:, slot, chunk, :], wlo[:, slot, chunk, :]
            else:
                dst_hi, dst_lo = (w[:, bass.ds(slot, 1), chunk, :].rearrange("p a n -> p (a n)") for w in (whi, wlo))
            free = None if m.loop else get(("slot free", slot))
            wait(act, at["raw", buf], free)
            hi = up(act.activation(dst_hi, raw[:, buf, :], ACT.Copy), c_whi)
            wait(by, hi, at["raw", buf])
            at["w"] = at["w", slot if isinstance(slot, int) else "loop"] = at["raw free", buf] = up(
                by.tensor_tensor(dst_lo, raw[:, buf, :], dst_hi.bitcast(f32), ALU.subtract), counter or c_wlo)

        def statistics():
            for t in range(GB):
                wait(dve, at["lnx", t], get("xhat"))
                a = up(dve.bn_stats(stats[:, t, :], lnx[:, t, :]), c_stat)
            for t in range(GB):
                wait(dve, a)
                fixed(dve)
                b = up(dve.bn_aggr(mv[:, t, :], stats[:, t, :]), c_stat)
            wait(pool, b)
            fixed(pool)
            c = up(pool.tensor_scalar(rstd[:, :], mv[:, :, 1], EPS, None, ALU.add), c_rstd)
            wait(pool, c)
            at["rstd"] = up(pool.tensor_tensor(rstd[:, :], rstd[:, :], power[:, :], ALU.pow), c_rstd)

        def normalise():
            for t in range(GB):
                wait(dve, at["rstd"])
                at["xhat"] = at["tile", t] = up(dve.tensor_scalar(
                    lnx[:, t, :], lnx[:, t, :], mv[:, t, 0:1], rstd[:, t:t + 1], ALU.subtract, ALU.mult), c_xhat)

        def fill_transpose(t, ln):
            wait(pe, at["tile", t] if ln else at["lnx", t], *bank_free[T_BANK + t])
            for c in range(KC):
                last = pe.transpose(ps[:, T_BANK + t, 128 * c:128 * c + 128], lnx[:, t, 128 * c:128 * c + 128], ident[:, :])
            at["ft", t] = up(last, c_ft if ln else c_fr)

        def fill_split(t, ln, buf, ln_name):
            hi, lo = (v[:, buf, :, T * t:T * t + T] for v in (xhi, xlo))
            src = ps[:, T_BANK + t, :].rearrange("p (c n) -> p c n", c=KC)
            free = at.get(("inputs free", buf))
            if ln:
                y = lnx[:, t, :].rearrange("p (c n) -> p c n", c=KC)
                g0, b0 = COL[ln_name + "_s"], COL[ln_name + "_b"]
                wait(act, at["ft", t])
                for c in range(KC):
                    last = act.activation(y[:, c, :], src[:, c, :], ACT.Identity, bias=cols[:, b0 + c:b0 + c + 1],
                                          scale=cols[:, g0 + c:g0 + c + 1])
                done = up(last, c_y)
                bank_free[T_BANK + t] = [done]
                wait(dve, done, free)
                a = up(dve.tensor_copy(hi, y), c_fhi)
                wait(pool, a, free)
                b = up(pool.tensor_tensor(lo, y, hi.bitcast(f32), ALU.subtract), c_flo)
                at["lnx free", t] = b
            else:
                at["lnx free", t] = at["ft", t]
                wait(act, at["ft", t], free)
                a = up(act.activation(hi, src, ACT.Copy), c_rhi)
                wait(dve, a, free)
                b = up(dve.tensor_tensor(lo, src, hi.bitcast(f32), ALU.subtract), c_rlo)
                bank_free[T_BANK + t] = [b]
            at["inputs", buf, t] = b
            at["inputs hi", buf, t] = a

        def project(phase, name, half, g_par, buf, bank, parts=(0, 1)):
            slot = UNITS[phase][name] % SLOTS
            if 0 in parts:
                wait(pe, *[at["inputs", buf, t] for t in (range(GB) if name != "v" else [half])], *bank_free[bank])
            for part in parts:
                if name == "v":
                    tok = slice(T * half, T * half + T)
                    todo = [(c, ps[:, bank, :], a[:, buf, c, tok], w[:, slot, c, :], 3 * c + n)
                            for c in range(2 * part, 2 * part + 2) for n, (a, w) in enumerate(((xhi, whi), (xhi, wlo), (xlo, whi)))]
                else:
                    o = slice(128 * (2 * half + part), 128 * (2 * half + part) + 128)
                    todo = [(c, ps[:, bank, GT * part:GT * part + GT], w[:, slot, c, o], a[:, buf, c, :], 3 * c + n)
                            for c in range(KC) for n, (w, a) in enumerate(((whi, xhi), (whi, xlo), (wlo, xhi)))]
                for c, dst, stationary, moving, n in todo:
                    last = pe.matmul(dst, stationary, moving, start=n == 0, stop=n == 3 * KC - 1)
            if 1 not in parts:
                return
            done = up(last, c_u)
            at["inputs free", buf] = at["slot free", slot] = done
            if name == "v":
                old = get(("v free", g_par))
                if phase == "D":
                    wait(act, done, old)
                    e = up(act.activation(vv[:, g_par, half, :], ps[:, bank, :], ACT.Copy), c_uv)
                else:
                    wait(dve, done, old)
                    e = up(dve.tensor_tensor(vv[:, g_par, half, :], ps[:, bank, :], brow[:, ROW_SLOT[phase + "_v"], :], ALU.add), c_ud)
            else:
                dst = (qT if name == "q" else kT)[:, g_par, 2 * half:2 * half + 2, :]
                wait(act, done, get(("qk free", g_par)))
                if phase == "D":
                    e = up(act.activation(dst, ps[:, bank, :].rearrange("p (c n) -> p c n", c=2), ACT.Copy), c_ua)
                else:
                    col = COL[f"{phase}_{name}"] + 2 * half
                    for k in range(2):
                        last = act.activation(dst[:, k, :], ps[:, bank, GT * k:GT * k + GT], ACT.Identity,
                                              bias=cols[:, col + k:col + k + 1])
                    e = up(last, c_ua)
            at[name, g_par] = e
            bank_free[bank] = [e]

        def unit_list(phase):
            if phase == "A":
                return [("q", 0, None), ("q", 1, None), ("k", 0, None), ("k", 1, None), ("v", 0, None), ("v", 1, None)]
            return [("k", 0, 0), ("k", 1, 0), ("v", 0, 0), ("v", 1, 0), ("q", 0, 1), ("q", 1, 1)]

        def mask_bias(phase, b, par):
            if phase == "B":
                wait(dve, at["mask", par], get(("mask bias free", par)))
                at["mask bias", par] = up(dve.tensor_scalar(mbias[:, par, :], msk[:, par, :], 1.0, 10000.0, ALU.subtract, ALU.mult), c_mb)
            if phase == "D":
                row = mrow[:, par, :]
                wait(dve, at["mask", par], get(("mask bias free", par)))
                a = at["mask free", par] = up(dve.tensor_scalar(mbias[:, par, :], row, 1.0, 3e38, ALU.subtract, ALU.mult), c_mb)
                wait(dve, a)
                at["mask bias", par] = up(dve.tensor_scalar(mbias[:, par, :], mbias[:, par, :], 4.0, None, ALU.mult), c_mb2)

        def period(phase, b, k, prev, cur=True, units=None, fills=(), weight=None, pieces=(), hidden=(), tight=False, put_off=None):
            par, gp, half = k % 2, (k // 2) % 2, k % 2
            pp = 1 - par
            pgp, phalf = ((k - 1) // 2) % 2, (k - 1) % 2
            P, Pp = prob[:, par, :], prob[:, pp, :]
            heads = lambda v: v.rearrange("p (h n) -> p h n", n=T)

            if prev:
                pph, pb = prev
                v_ready = at["v", pgp]
                wait(sp, get(("stored", pp)))
                at["res", pp] = up(sp.dma_start(res[:, pp, :], xs["ABCD".index(pph)][bass.ds(pb * T, T), :]), c_res[pp], 16)
            for t in range(GB if fills else 0):
                src, row, ln_name, buf = fills
                load_tile(t, src, row + t * T, c_lnx if ln_name else c_rawx)
            if weight:
                load_weight(weight[0], weight[2], k % STG)
            spare = [n for n in range(STG) if n != k % STG]
            for piece, buf in zip(pieces, spare):
                load_weight(*piece, buf)

            def split_piece(n):
                if n < len(pieces):
                    split_weight(pieces[n][0] % SLOTS, pieces[n][1], spare[n % 3])
                    if n + 3 < len(pieces):
                        load_weight(*pieces[n + 3], spare[n])

            def ride(place):
                if place in hidden:
                    hidden[place]()

            if cur:
                wait(pe, at["q", gp], at["k", gp], *(f for j in range(4) for f in bank_free[j]))
                for c in range(KC):
                    for j in range(4):
                        r, tk = slice(32 * j, 32 * j + 32), slice(T * half, T * half + T)
                        last = pe.matmul(ps[:, S_BANK + j, T * c:T * c + T], qT[r, gp, c, tk], kT[r, gp, c, tk], start=True, stop=True)
                scores = up(last, c_scores)
                if half == 1:
                    at["qk free", gp] = scores
                mask_bias(phase, b, par)
                for h in range(2):
                    wait(dve, scores, at["mask bias", par if phase != "A" else 0], get(("prob free", par)), const)
                    other = (msk[:, par if phase == "B" else 0, :] if phase != "D" else mbias[:, par, :])
                    for c in (2 * h, 2 * h + 1):
                        last = dve.scalar_tensor_tensor(
                            heads(P[:, 512 * c:512 * c + 512]), ps[:, S_BANK:S_BANK + 4, T * c:T * c + T], SCALE,
                            other.unsqueeze(1).to_broadcast([128, 4, T]), ALU.mult, ALU.add if phase == "D" else ALU.mult)
                    at["masked", h] = up(last, c_masked)
                for j in range(4):
                    bank_free[j] = [at["masked", 1]]
                if phase == "D":
                    at["mask bias free", par] = at["masked", 1]
                if phase != "D":
                    at["mask free", par if phase == "B" else 0] = at["masked", 1]
                if phase != "D":
                    for h in range(2):
                        s = slice(1024 * h, 1024 * h + 1024)
                        wait(pool, at["masked", h], at["mask bias", par if phase == "B" else 0])
                        mb = mbias[:, par if phase == "B" else 0, :]
                        at["masked", h] = up(pool.tensor_tensor(heads(P[:, s]), heads(P[:, s]),
                                                                mb.unsqueeze(1).to_broadcast([128, 8, T]), ALU.add), c_biased)
                    at["mask bias free", par if phase == "B" else 0] = at["masked", 1]

            if cur and phase != "A" and not (isinstance(b, int) and b == NB - 1):
                load_mask(phase, b, k)

            def row_max(h):
                wait(dve, at["masked", h], get(("max free", par)))
                at["max", h] = up(dve.tensor_reduce(negmax[:, par, 8 * h:8 * h + 8], heads(P[:, 1024 * h:1024 * h + 1024]),
                                                    AX.X, ALU.max, negate=True), c_max)

            def exps(q):
                wait(act, at["max", q // 2], at["masked", q // 2], get(("total free", par)))
                for s in range(4 * q, 4 * q + 4):
                    last = act.activation(P[:, T * s:T * s + T], P[:, T * s:T * s + T], ACT.Exp,
                                          bias=negmax[:, par, s:s + 1], accum_out=total[:, par, s:s + 1])
                at["exp"] = at["exp", q] = up(last, c_exp)

            def probabilities(h):
                wait(dve, at["exp", 2 * h + 1])
                hs = slice(8 * h, 8 * h + 8)
                r = at["total free", par] = up(dve.reciprocal(rtotal[:, par, hs], total[:, par, hs]), c_rt)
                wait(dve, r)
                half = heads(P[:, 1024 * h:1024 * h + 1024])
                rb = rtotal[:, par, hs].unsqueeze(2).to_broadcast([128, 8, T])
                at["prob", par, h] = up(dve.tensor_tensor(half, half, rb, ALU.mult), c_prob)

            def unit(n, bank, parts=(0, 1)):
                if units:
                    uph, lst, ugp = units
                    if n >= len(lst) or lst[n] is None:
                        return
                    name, hf, buf = lst[n]
                    project(uph, name, hf, ugp, ugp if buf is None else buf, bank, parts)

            def transpose_prob(c):
                bank = T_BANK + c % 2
                wait(pe, at["prob", pp, c // 2], *bank_free[bank])
                for j in range(4):
                    last = pe.transpose(ps[:, bank, T * j:T * j + T], Pp[:, T * (4 * c + j):T * (4 * c + j) + T], ident[:, :])
                done = up(last, c_tr)
                if c == KC - 1:
                    at["prob free", pp] = done
                if c % 2 == 0:
                    wait(act, done, get(("probT free", 0)))
                    e = up(act.activation(probT[:, 0, :], ps[:, bank, :], ACT.Copy), c_pta)
                else:
                    wait(dve, done, get(("probT free", 1)))
                    e = up(dve.tensor_copy(probT[:, 1, :], ps[:, bank, :]), c_ptd)
                bank_free[bank] = [e]
                at["probT", c % 2] = e

            def times_v(c):
                wait(pe, at["probT", c % 2], *([v_ready] + bank_free[0] if c == 0 else []))
                for j in range(4):
                    o = (4 * c + j) * HD
                    last = pe.matmul(ps[32 * j:32 * j + 32, 0, T * c:T * c + T], vv[:, pgp, phalf, o:o + HD],
                                     probT[:, c % 2, T * j:T * j + T], start=True, stop=True)
                at["pv"] = at["probT free", c % 2] = up(last, c_pv)
                if c == KC - 1 and phalf == 1:
                    at["v free", pgp] = at["pv"]

            def context_split():
                wait(act, at["pv"], get("ctx free"))
                a = up(act.activation(chi[:, 0, :], ps[:, 0, :], ACT.Copy), c_chi)
                wait(dve, a, get("ctx free"))
                at["ctx"] = up(dve.tensor_tensor(clo[:, 0, :], ps[:, 0, :], chi[:, 0, :].bitcast(f32), ALU.subtract), c_clo)
                bank_free[0] = [at["ctx"]]

            normal = bool(fills) and fills[2] is not None
            unit(0, U_BANK)
            ride("start")
            if normal:
                statistics()
            if prev:
                transpose_prob(0)
                transpose_prob(1)
            if cur and not tight:
                row_max(0)
                exps(0)
            unit(1, U_BANK + 1)
            if prev:
                times_v(0)
                times_v(1)
                transpose_prob(2)
                transpose_prob(3)
            if cur and tight:
                row_max(0)
            if cur and not tight:
                row_max(1)
            if prev and pph != "D":
                wait(pool, at["res", pp], const)
                resb = up(pool.tensor_tensor(res[:, pp, :], res[:, pp, :], brow[:, ROW_SLOT[pph + "_o"], :], ALU.add), c_resb)
            if normal:
                normalise()
            if cur and not tight:
                exps(1)
            ride("middle")
            unit(2, U_BANK, parts=(0,))
            if prev:
                times_v(2)
                times_v(3)
                context_split()
                ride("after context")
            unit(2, U_BANK, parts=(1,))
            if cur and tight:
                exps(0)
                row_max(1)
                exps(1)
                split_piece(0)
            if cur:
                exps(2)
            for t in range(GB if fills else 0):
                fill_transpose(t, normal)
                fill_split(t, normal, fills[3], fills[2])
            if cur:
                probabilities(0)
                exps(3)
            if prev:
                ride("before output")
                slot = UNITS[pph]["o"] % SLOTS
                wait(pe, at["ctx"], *bank_free[U_BANK + 1])
                n = 0
                for c in range(KC):
                    cs = slice(T * c, T * c + T)
                    for a, w in ((chi, whi), (chi, wlo), (clo, whi)):
                        last = pe.matmul(ps[:, U_BANK + 1, :], a[:, 0, cs], w[:, slot, c, :], start=n == 0, stop=n == 3 * KC - 1)
                        n += 1
                done = at["ctx free"] = at["slot free", slot] = up(last, c_o)
                if pph != "D":
                    wait(dve, done, resb)
                    e = up(dve.tensor_tensor(res[:, pp, :], ps[:, U_BANK + 1, :], res[:, pp, :], ALU.add), c_x)
                else:
                    wait(dve, done, at["res", pp])
                    e = up(dve.scalar_tensor_tensor(res[:, pp, :], ps[:, U_BANK + 1, :], gatec[:, 1:2], res[:, pp, :],
                                                    ALU.mult, ALU.add), c_x)
                bank_free[U_BANK + 1] = [e]
                wait(sp, e)
                at["stored", pp] = up(sp.dma_start(xs["ABCD".index(pph) + 1][bass.ds(pb * T, T), :], res[:, pp, :]), c_store[pp], 16)
            if cur:
                probabilities(1)
                at["max free", par] = at["exp"]
            splits = [lambda n=n: split_piece(n) for n in range(1, len(pieces))]
            if weight:
                splits.append(lambda: split_weight(weight[1], weight[2], k % STG))
            if put_off is None:
                for split in splits:
                    split()
            else:
                put_off += splits

        def load_mask(phase, b, k):
            p, row = (k + 1) % 2, bass.ds((b + 1) * T, T)
            wait(sp, get(("mask free", p)))
            if phase == "B":
                ins = sp.dma_start(msk[:, p, :], mask_b[row, :])
            else:
                ins = sp.dma_start(mrow[:, p, :], mask_d[:, row].to_broadcast([128, T]))
            at["mask", p] = up(ins, c_mload[p], 16)

        def weight_now(units, chunks=range(KC)):
            todo = [(u, c) for u in units for c in chunks]
            for n, (u, c) in enumerate(todo):
                load_weight(u, c, n % STG)
                split_weight(u % SLOTS, c, n % STG)

        def attention(phase, first_prev, last_units, kv, q, next_kv, weights_from, last_fills, last_steps=({}, {})):
            lst = unit_list(phase)

            def step(b, k, i=None):
                odd = k % 2
                gp_next = (k // 2 + 1) % 2
                fills = ()
                if odd:
                    buf = (k // 2) % 2 if phase == "A" else 0
                    fills = (kv[0], (b - 1 + 2 * GB) * T, kv[1], buf)
                elif phase != "A":
                    fills = (q[0], (b + GB) * T, q[1], 1)
                weight = None
                if weights_from is not None:
                    u = b // 4 if i is None else i + (k == 0)
                    weight = (u + weights_from, u + weights_from % SLOTS, k)
                return dict(units=(phase, lst[3 * odd:3 * odd + 3], gp_next), fills=fills, weight=weight)

            if first_prev is None:
                pv, o, tr, sc, ex, rt = m.now(c_pv, c_o, c_tr, c_scores, c_exp, c_rt)
                at.update({("probT free", 0): pv, ("probT free", 1): pv, "ctx free": o, ("prob free", 1): tr,
                           ("v free", 1): pv, ("qk free", 1): sc, ("max free", 1): ex, ("total free", 1): rt})
                at["stored", 0], at["stored", 1] = m.now(*c_store)
                finished = {U_BANK + 1: m.now(c_x), 0: m.now(c_clo), T_BANK: m.now(c_pta), T_BANK + 1: m.now(c_ptd)}
            if phase == "B":
                at["mask free", 1], at["mask bias free", 1] = m.now(c_masked, c_biased)
            if phase == "D":
                at["mask bias free", 1], = m.now(c_masked)
                at["mask free", 1], = m.now(c_mb)
                load_mask("D", -1, 3)

            own = at["w"]
            period(phase, 0, 0, first_prev, **step(0, 0))
            if first_prev is None:
                for bank, marks in finished.items():
                    bank_free[bank] = bank_free[bank] + marks
            if weights_from is not None:
                for slot in range(weights_from % SLOTS, weights_from % SLOTS + 4):
                    wait(act, get(("slot free", slot)))
                    wait(pool, get(("slot free", slot)))

            def body(i):
                for k in (1, 2, 3, 4):
                    b = i * 4 + k
                    period(phase, b, k % 4, (phase, i * 4 + (k - 1)), **step(b, k % 4, i))

            wait(pe, own)
            m.run("attention", 3, body)
            split_in_loop = at["w"]
            kw = step(13, 1)
            kw["fills"] = next_kv
            held = None
            if phase == "D":
                held = kw["units"][1][0]
                kw["units"] = (phase, [None] + kw["units"][1][1:], 1)
            period(phase, 13, 1, (phase, 12), **kw)
            if phase == "A":
                wait(sp, *m.now(c_ud))
                b_v = load_bias_row("B_v")
                wait(dve, b_v)
            for b in (14, 15):
                kw = step(b, b % 4)
                kw["units"], kw["fills"] = (phase, [held], 1) if held and b == 14 else None, last_fills[b - 14]
                if last_units:
                    wait(pe, split_in_loop)
                    kw["units"] = (last_units, unit_list(last_units)[3 * (b - 14):3 * (b - 14) + 3], 0)
                period(phase, b, b % 4, (phase, b - 1), **kw, **last_steps[b - 14], tight=phase != "A")

        hidden_x, hidden_w = (v[:, :, :, :].rearrange("p g c n -> p (g c n)") for v in (qT, kT))
        hx = lambda n: hidden_x[:, 512 * (n % 4):512 * (n % 4) + 512]
        hw = lambda n: hidden_w[:, 512 * (n % 4):512 * (n % 4) + 512]

        def pair(g, gp, jp, cur=True, ahead=True, last=True):
            bank = U_BANK + jp % 2
            if cur:
                slot = W1_UNIT[jp // 2] % SLOTS
                if cur is not OUT:
                    wait(pe, at["inputs", gp, 0], at["inputs", gp, 1], *bank_free[bank], None if m.loop else get(("w", slot)))
                for e in {True: (0, 1), FIRST: (0,), SECOND: (1,), OUT: ()}[cur]:
                    o = slice(128 * (2 * (jp % 2) + e), 128 * (2 * (jp % 2) + e) + 128)
                    n = 0
                    for c in range(KC):
                        for w, a in ((whi, xhi), (whi, xlo), (wlo, xhi)):
                            mm = pe.matmul(ps[:, bank, GT * e:GT * e + GT], w[:, slot, c, o], a[:, gp, c, :],
                                           start=n == 0, stop=n == 3 * KC - 1)
                            n += 1
                if cur is FIRST:
                    return
                if cur is not OUT:
                    at["hidden"] = at["slot free", slot] = at["inputs free", gp] = up(mm, c_h)
                if cur is SECOND:
                    return
                h = at["hidden"]
            if ahead:
                q = (jp - 1) % 4
                wait(act, at["tanh in", q])
                th = up(act.activation(hw(q), hw(q), ACT.Tanh, scale=GELU_A * GELU_C), c_th)
            if cur:
                wait(act, h, get(("hx free", jp % 4)))
                for e in range(2):
                    col = COL["b1"] + 2 * jp + e
                    ins = act.activation(hx(jp)[:, GT * e:GT * e + GT], ps[:, bank, GT * e:GT * e + GT], ACT.Identity,
                                         bias=cols[:, col:col + 1])
                x_ = up(ins, c_hx)
                bank_free[bank] = [x_]
                wait(act, x_, get(("hw free", jp % 4)))
                sq = up(act.activation(hw(jp), hx(jp), ACT.Square), c_sq)
            if ahead:
                wait(dve, th, at["hx", q])
                y = up(dve.scalar_tensor_tensor(hw(q), hw(q), 1.0, hx(q), ALU.add, ALU.mult), c_gy)
                at["hx free", q] = y
                gb = jp % 2
                wait(dve, y, get(("gelu free", gb)))
                ghi = up(dve.tensor_scalar(chi[:, gb, :], hw(q), 0.5, None, ALU.mult), c_ghi)
            if cur:
                wait(dve, sq, x_)
                at["tanh in", jp % 4] = up(dve.scalar_tensor_tensor(hw(jp), hw(jp), 1.0 / GELU_A, hx(jp), ALU.add, ALU.mult), c_in)
                at["hx", jp % 4] = x_
            if ahead:
                wait(dve, ghi, get(("gelu free", gb)))
                at["gelu", gb] = at["hw free", q] = up(dve.scalar_tensor_tensor(
                    clo[:, gb, :], hw(q), 0.5, chi[:, gb, :].bitcast(f32), ALU.mult, ALU.subtract), c_glo)
            if last:
                j2, g2 = (jp - 2) % NPAIR, gp if jp >= 2 else 1 - gp
                slot, gb = W2_UNIT[j2 // 2] % SLOTS, (jp - 1) % 2
                for t in range(GB):
                    acc = 2 * (1 - g2) + t
                    wait(pe, at["gelu ready", gb], *(bank_free[acc] if j2 == 0 else []), None if m.loop else get(("w", slot)))
                    n = 0
                    for e in range(2):
                        tok = slice(GT * e + T * t, GT * e + T * t + T)
                        for a, w in ((chi, whi), (chi, wlo), (clo, whi)):
                            mm = pe.matmul(ps[:, acc, :], a[:, gb, tok], w[:, slot, 2 * (j2 % 2) + e, :],
                                           start=j2 == 0 and n == 0, stop=j2 == NPAIR - 1 and n == 5)
                            n += 1
                at["gelu free", gb] = at["slot free", slot] = up(mm, c_w2)
            if ahead:
                at["gelu ready", jp % 2] = at["gelu", jp % 2]

        def mlp_out(g, g2):
            done = at["gelu free", 0]
            for t in range(GB):
                wait(pool, at["res", t])
                rb = up(pool.tensor_tensor(res[:, t, :], res[:, t, :], brow[:, ROW_SLOT["C_o"], :], ALU.add), c_resb)
                wait(dve, done, rb)
                e = up(dve.tensor_tensor(res[:, t, :], ps[:, 2 * (1 - g2) + t, :], res[:, t, :], ALU.add), c_x)
                bank_free[2 * (1 - g2) + t] = [e]
                wait(sp, e)
                at["stored", t] = up(sp.dma_start(xs[3][bass.ds(g * GT + t * T, T), :], res[:, t, :]), c_store[t], 16)

        def mlp_residual(g):
            for t in range(GB):
                wait(sp, at["stored", t])
                at["res", t] = up(sp.dma_start(res[:, t, :], xs[2][bass.ds(g * GT + t * T, T), :]), c_res[t], 16)

        def group(g, gp, fills, start=0, weights=None):
            src, row, ln_name, buf = fills
            for jp in range(start, NPAIR):
                if jp == 0:
                    mlp_residual(g - 1)
                    for t in range(GB):
                        load_tile(t, src, row + t * T, c_lnx)
                pair(g, gp, jp)
                if jp == 1:
                    mlp_out(g - 1, 1 - gp)
                if jp == 2:
                    statistics()
                if jp == 3:
                    normalise()
                if jp == max(4, start):
                    for t in range(GB):
                        fill_transpose(t, True)
                        fill_split(t, True, buf, ln_name)
                if weights and jp in weights:
                    weight_now([weights[jp]])

        for t in range(GB):
            load_tile(t, x, t * T, c_lnx)
        for dst, src in ((ident[:, :], ident_in), (cols[:, :], columns)):
            first = up(sp.dma_start(dst, src), c_first, 16)
        for c in range(KC):
            load_weight(0, c, c)
        whole = [up(sp.dma_start(prob[:, u - 1, :].rearrange("p (c n) -> p c n", c=KC), weights[u].rearrange("c p n -> p c n")),
                    c_start[u - 1], 16) for u in (1, 2)]
        for dst, src in ((gatec[:, 0:1], gate.to_broadcast([128, 1])), (msk[:, 0, :], mask_a)):
            up(sp.dma_start(dst, src), c_const, 16)
        for name in ("A_v", "A_o", "B_o"):
            const = load_bias_row(name)

        def split_start(unit, by, counter):
            src = prob[:, unit - 1, :].rearrange("p (c n) -> p c n", c=KC)
            for c in range(KC):
                wait(act, whole[unit - 1])
                hi = up(act.activation(whi[:, unit, c, :], src[:, c, :], ACT.Copy), c_whi)
                wait(by, hi, whole[unit - 1])
                at["w"] = at["w", unit] = at["prob free", unit - 1] = up(
                    by.tensor_tensor(wlo[:, unit, c, :], src[:, c, :], whi[:, unit, c, :].bitcast(f32), ALU.subtract), counter)

        wait(act, first)
        wait(pe, first)
        statistics()
        normalise()
        for c in range(KC):
            split_weight(0, c, c, by=dve, counter=c_wld)
        for t in range(GB):
            fill_transpose(t, True)
            fill_split(t, True, 0, "ln1")
        for t in range(GB):
            load_tile(t, x, (GB + t) * T, c_lnx)
        for c in range(KC):
            load_weight(3, c, c)
        wait(dve, const)
        at["mask bias", 0] = up(dve.tensor_scalar(mbias[:, 0, :], msk[:, 0, :], 1.0, 10000.0, ALU.subtract, ALU.mult), c_small)
        split_start(1, pool, c_wlo)
        statistics()
        split_start(2, dve, c_wld)
        for n, (name, hf, _) in enumerate(unit_list("A")):
            wait(pe, at["w", UNITS["A"][name]])
            project("A", name, hf, 0, 0, U_BANK + n % 2)
            if (name, hf) == ("q", 1):
                normalise()
            if (name, hf) == ("k", 1):
                for t in range(GB):
                    fill_transpose(t, True)
                    fill_split(t, True, 1, "ln1")
        for c in range(KC):
            split_weight(3, c, c)
        wait(act, const)
        wait(act, table)
        tanh = up(act.activation(gatec[:, 1:2], gatec[:, 0:1], ACT.Tanh), c_small)
        wait(dve, tanh)

        attention("A", None, "B", (x, "ln1"), None, (enc, 0, None, 0), 4, [(xs[1], 0, "ln2", 1), (enc, GT, None, 0)])
        load_mask("B", -1, 3)
        def hidden_first(jp, part):
            if jp in (0, 2) and part is OUT:
                wait(act, get(("qk free", jp // 2)))
            pair(0, 0, jp, cur=part, ahead=False, last=False)

        later = []
        attention("B", ("A", NB - 1), None, (enc, None), (xs[1], "ln2"), (xs[2], 0, "ln3", 0), 8, [(), ()],
                  [dict(hidden={"start": lambda: hidden_first(0, FIRST), "middle": lambda: hidden_first(0, SECOND),
                                "after context": lambda: hidden_first(0, OUT)},
                        pieces=[(12, c) for c in range(KC)]),
                   dict(hidden={"start": lambda: hidden_first(1, FIRST), "middle": lambda: hidden_first(1, SECOND),
                                "after context": lambda: hidden_first(1, OUT)},
                        pieces=[(14, c) for c in range(KC)], put_off=later)])
        for t in range(GB):
            load_tile(t, xs[2], GT + t * T, c_lnx)
        period("B", NB, 0, ("B", NB - 1), cur=False,
               hidden={"start": lambda: (hidden_first(2, FIRST), hidden_first(2, SECOND)),
                       "middle": lambda: (pair(0, 0, 1, cur=False, last=False), hidden_first(2, OUT),
                                          pair(0, 0, 3, ahead=False, last=False)),
                       "after context": lambda: [split() for split in later],
                       "before output": lambda: pair(0, 0, 2, cur=False, ahead=False)})
        wait(sp, *m.now(c_resb))
        wait(pool, load_bias_row("C_o"))
        at["gelu free", 0] = at["ctx free"]
        pair(0, 0, 2, cur=False, last=False)
        pair(0, 0, 4, ahead=False, last=False)
        statistics()
        pair(0, 0, 3, cur=False)
        normalise()
        weight_now([13], (0, 1))
        pair(0, 0, 4, cur=False)
        weight_now([13], (2, 3))

        group(0, 0, (xs[2], GT, "ln3", 1), start=5, weights={6: 15})
        wait(pe, at["w"])
        at["stored", 0], at["stored", 1] = m.now(*c_store)

        def body(i):
            for k in (1, 2):
                group(i * 2 + k, k % 2, (xs[2], (i * 2 + (k + 1)) * GT, "ln3", (k + 1) % 2))

        m.run("hidden", 3, body)
        group(NG - 1, 1, (enc, 0, "lna", 0), weights={3: 16, 4: 17, 5: 18, 7: 19})
        mlp_residual(NG - 1)
        for t in range(GB):
            load_tile(t, xs[3], t * T, c_rawx)
        def project_first(n):
            name, hf, buf = unit_list("D")[n]
            wait(pe, at["w", UNITS["D"][name] % SLOTS])
            project("D", name, hf, 0, buf, U_BANK + n % 2)

        pair(NG, 0, 0, cur=False)
        project_first(0)
        pair(NG, 0, 1, cur=False, ahead=False)
        mlp_out(NG - 1, 1)

        for t in range(GB):
            fill_transpose(t, False)
            fill_split(t, False, 1, None)
        for n in range(1, 6):
            project_first(n)
        for t in range(GB):
            load_tile(t, enc, GT + t * T, c_lnx)
        statistics()
        normalise()
        for t in range(GB):
            fill_transpose(t, True)
            fill_split(t, True, 0, "lna")
        wait(pe, at["w"])
        attention("D", None, None, (enc, "lna"), (xs[3], None), (), None, [(), ()])
        period("D", NB, 0, ("D", NB - 1), cur=False)
        for p in range(2):
            wait(sp, at["stored", p])


def kernel(x, ctx_2048, mask_1x1xSxS2_fc1, mask_Bx1xSxS2_ff1, mask_BxS2_bf1, **p):
    import numpy as np
    import concourse.bacc as bacc
    from concourse.bass_utils import run_bass_kernel_spmd

    a = {k.removeprefix("L0_xattn_").replace("L1_xattn_", "L1_"): np.asarray(v) for k, v in p.items()}

    def unit(w, r, c):
        return w[H * r:H * r + H, H * c:H * c + H].reshape(KC, 128, H)

    blocks = [unit(a["w_qkv"], 0, 0), unit(a["w_qkv"], 0, 1), unit(a["w_qkv"], 0, 2), unit(a["w_ao"], 0, 0),
              unit(a["w_q"], 0, 0), unit(a["w_kv"], 0, 0), unit(a["w_kv"], 0, 1), unit(a["w_co"], 0, 0)]
    for j in range(4):
        blocks += [unit(a["w1"], 0, j), unit(a["w2"], j, 0)]
    blocks += [unit(a[f"L1_W{n}"].T, 0, 0) for n in "kvqo"]
    b_qkv, b_kv = a["b_qkv"], a["b_kv"]
    columns = np.concatenate([v.reshape(-1, 128).T for v in (
        a["ln1_s"], a["ln1_b"], a["ln2_s"], a["ln2_b"], a["ln3_s"], a["ln3_b"], a["L1_ln_gamma"], a["L1_ln_beta"],
        b_qkv[:H], b_qkv[H:2 * H], a["b_q"], b_kv[:H], a["b1"])], axis=1)
    rows = np.stack([b_qkv[2 * H:], a["b_ao"], b_kv[H:], a["b_co"], a["b2"]])
    arrays = dict(
        x=np.asarray(x).reshape(NB * T, H), enc=np.asarray(ctx_2048).reshape(NB * T, H),
        mask_a=np.asarray(mask_1x1xSxS2_fc1).reshape(T, T), mask_b=np.asarray(mask_Bx1xSxS2_ff1).reshape(NB * T, T),
        mask_d=np.asarray(mask_BxS2_bf1).reshape(1, NB * T).view(np.uint8),
        weights=np.stack(blocks), columns=columns, rows=rows, gate=a["L1_gate"].reshape(1, 1),
        ident=np.eye(128, dtype=np.float32))
    nc = bacc.Bacc("TRN2", target_bir_lowering=False, num_devices=1, dynamic_dma_scratch_size=1024)
    arrays = {f"{k}_in": np.ascontiguousarray(v) for k, v in arrays.items()}
    args = [nc.dram_tensor(k, v.shape, mybir.dt.from_np(v.dtype), kind="ExternalInput").ap() for k, v in arrays.items()]
    args.append(nc.dram_tensor("result", (NB * T, H), mybir.dt.float32, kind="ExternalOutput").ap())
    build(nc, *args)
    r = run_bass_kernel_spmd(nc, [arrays], core_ids=[0])
    return r.results[0]["result"].reshape(NB, T, H)
```
